# Optimizing a Trainium2 kernel written in Bass

```python
import numpy as np
import jax
import jax.numpy as jnp

def _softmax(x, axis=-1):
    return jax.nn.softmax(x, axis=axis)

def _gelu(x):
    return jax.nn.gelu(x, approximate=True)

def _silu(x):
    return jax.nn.silu(x)

def _sigmoid(x):
    return jax.nn.sigmoid(x)

def _layernorm(x, axis=-1, eps=1e-05):
    m = jnp.mean(x, axis=axis, keepdims=True)
    v = jnp.var(x, axis=axis, keepdims=True)
    return (x - m) / jnp.sqrt(v + eps)

def _scatter_add(tgt, idx, src, axis=0):
    return tgt.at[idx].add(src)

def _segment_sum(src, seg, n):
    return jax.ops.segment_sum(src, seg, n)
kernel_name = 'mk_adaln_ffn_d2_seqx_r8_70a462'

def setup_inputs(seed: int=0):
    np.random.seed(seed)
    _w = jnp.asarray

    def _rec_inputs():
        import jax
        import jax.numpy as jnp
        _rk = jax.random.key(seed)
        x = -7.109e-05 + 0.9999 * jax.random.normal(jax.random.fold_in(_rk, 1), (128, 32, 256), jnp.float32)
        _lenS = 32 - jax.random.randint(jax.random.fold_in(_rk, 7), (128,), 0, max(1, 32 // 4) + 1, jnp.int32)
        _lenS2 = 32 - jax.random.randint(jax.random.fold_in(_rk, 8), (128,), 0, max(1, 32 // 4) + 1, jnp.int32)
        itok_B_1_198 = jax.random.randint(jax.random.fold_in(_rk, 11), (128,), 1, 199, jnp.int32)
        itok_Bx257_0_4111 = jax.random.randint(jax.random.fold_in(_rk, 12), (128, 257), 0, 514, jnp.int32)
        itok_B_37_3939 = jax.random.randint(jax.random.fold_in(_rk, 13), (128,), 37, 3940, jnp.int32)
        return (x, itok_B_1_198, itok_Bx257_0_4111, itok_B_37_3939)
    x, itok_B_1_198, itok_Bx257_0_4111, itok_B_37_3939 = _rec_inputs()

    def _L0_cond_setup():
        import jax, jax.numpy as jnp
        import numpy as np
        B, C, T = (128, 32, 256)
        S, D = (200, 32)
        key = jax.random.key(seed)
        k1, k2, k3 = jax.random.split(key, 3)
        x = jax.random.normal(k1, (B, C, T), dtype=jnp.float32)
        conditions = jax.random.randint(k2, (B,), 0, S, dtype=jnp.int64)
        weights = jax.random.normal(k3, (S, C, D), dtype=jnp.float32) / jnp.sqrt(jnp.float32(C))
        return {'x': x, 'conditions': conditions, 'weights': weights}
    _L0_cond_all = _L0_cond_setup()
    _L0_cond_in = {k: v for k, v in _L0_cond_all.items() if k in ('weights',)}
    del _L0_cond_all

    def _L0_ffn_setup():
        import jax, jax.numpy as jnp
        import numpy as np
        TOP_K = 2
        SCALING = 2.0
        key = jax.random.key(seed)
        ks = jax.random.split(key, 10)
        B, S, H, I, E, R = (1, 64, 256, 128, 8, 16)
        w = 1.0 / np.sqrt(H)
        inp = {'x': jax.random.normal(ks[0], (B, S, H), jnp.float32), 'gate_weight': jax.random.normal(ks[1], (E, H), jnp.float32) * w, 'gate_lora_A': jax.random.normal(ks[2], (R, H), jnp.float32) * 0.02, 'gate_lora_B': jax.random.normal(ks[3], (E, R), jnp.float32) * 0.02, 'gate_up_proj': jax.random.normal(ks[4], (E, H, 2 * I), jnp.float32) * w, 'down_proj': jax.random.normal(ks[5], (E, I, H), jnp.float32) * (1.0 / np.sqrt(I)), 'gup_lora_A': jax.random.normal(ks[6], (E, R, H), jnp.float32) * 0.02, 'gup_lora_B': jax.random.normal(ks[7], (E, 2 * I, R), jnp.float32) * 0.02, 'down_lora_A': jax.random.normal(ks[8], (E, R, I), jnp.float32) * 0.02, 'down_lora_B': jax.random.normal(ks[9], (E, H, R), jnp.float32) * 0.02}
        return inp
    _L0_ffn_all = _L0_ffn_setup()
    _L0_ffn_in = {k: v for k, v in _L0_ffn_all.items() if k in ('gate_weight', 'gate_lora_A', 'gate_lora_B', 'gate_up_proj', 'down_proj', 'gup_lora_A', 'gup_lora_B', 'down_lora_A', 'down_lora_B')}
    del _L0_ffn_all

    def _L1_cond_setup():
        import jax, jax.numpy as jnp
        import numpy as np
        H, G, HD = (8, 4, 32)
        GSZ = H // G
        BLOCK = 16
        WINDOW = 128
        SCALE = 256.0 ** (-0.5)
        EPS = 1e-06
        THETA = 10000.0
        B, T, D = (16, 4, 256)
        NBLK = 257

        def _rms(x, scale):
            var = jnp.mean(x * x, axis=-1, keepdims=True)
            return x * jax.lax.rsqrt(var + EPS) * (1.0 + scale)

        def _rope(x, pos):
            half = HD // 2
            inv = 1.0 / THETA ** (jnp.arange(half, dtype=jnp.float32) / half)
            ang = pos[:, :, None].astype(jnp.float32) * inv
            cos = jnp.cos(ang)[:, None, :, :]
            sin = jnp.sin(ang)[:, None, :, :]
            x1, x2 = (x[..., :half], x[..., half:])
            return jnp.concatenate([x1 * cos - x2 * sin, x2 * cos + x1 * sin], axis=-1)
        key = jax.random.key(seed)
        ks = jax.random.split(key, 10)
        inv_d = 1.0 / np.sqrt(D)
        return {'x': jax.random.normal(ks[0], (B, T, D), jnp.float32), 'Wq': jax.random.normal(ks[1], (H * HD, D), jnp.float32) * inv_d, 'Wk': jax.random.normal(ks[2], (G * HD, D), jnp.float32) * inv_d, 'Wv': jax.random.normal(ks[3], (G * HD, D), jnp.float32) * inv_d, 'Wo': jax.random.normal(ks[4], (D, H * HD), jnp.float32) * inv_d, 'q_norm_scale': jax.random.normal(ks[5], (HD,), jnp.float32) * 0.02, 'k_norm_scale': jax.random.normal(ks[6], (HD,), jnp.float32) * 0.02, 'k_blocks': jax.random.normal(ks[7], (B * NBLK, G, BLOCK, HD), jnp.float32), 'v_blocks': jax.random.normal(ks[8], (B * NBLK, G, BLOCK, HD), jnp.float32), 'block_tables': jnp.arange(B * NBLK, dtype=jnp.int32).reshape(B, NBLK), 'kv_lens': jax.random.randint(ks[9], (B,), 0, 512, dtype=jnp.int32)}
    _L1_cond_all = _L1_cond_setup()
    _L1_cond_in = {k: v for k, v in _L1_cond_all.items() if k in ('Wq', 'Wk', 'Wv', 'Wo', 'q_norm_scale', 'k_norm_scale', 'k_blocks', 'v_blocks')}
    del _L1_cond_all

    def _L1_ffn_setup():
        import jax, jax.numpy as jnp
        import numpy as np
        DIM = 256
        HIDDEN = 1024
        NUM_EXPERTS = 2
        BATCH, SEQ = (4, 128)
        key = jax.random.key(seed)
        k1, k2, k3, k4 = jax.random.split(key, 4)
        x = jax.random.normal(k1, (BATCH, SEQ, DIM), dtype=jnp.float32)
        w_router = jax.random.normal(k2, (NUM_EXPERTS, DIM), dtype=jnp.float32) * (1.0 / np.sqrt(DIM))
        w_fc = jax.random.normal(k3, (NUM_EXPERTS, HIDDEN, DIM), dtype=jnp.float32) * (1.0 / np.sqrt(DIM))
        w_proj = jax.random.normal(k4, (NUM_EXPERTS, DIM, HIDDEN), dtype=jnp.float32) * (1.0 / np.sqrt(HIDDEN))
        return {'x': x, 'w_router': w_router, 'w_fc': w_fc, 'w_proj': w_proj}
    _L1_ffn_all = _L1_ffn_setup()
    _L1_ffn_in = {k: v for k, v in _L1_ffn_all.items() if k in ('w_router', 'w_fc', 'w_proj')}
    del _L1_ffn_all
    return {'x': x, 'itok_B_1_198': itok_B_1_198, 'itok_Bx257_0_4111': itok_Bx257_0_4111, 'itok_B_37_3939': itok_B_37_3939, 'L0_cond_weights': _L0_cond_in['weights'], 'L0_ffn_gate_weight': _L0_ffn_in['gate_weight'], 'L0_ffn_gate_lora_A': _L0_ffn_in['gate_lora_A'], 'L0_ffn_gate_lora_B': _L0_ffn_in['gate_lora_B'], 'L0_ffn_gate_up_proj': _L0_ffn_in['gate_up_proj'], 'L0_ffn_down_proj': _L0_ffn_in['down_proj'], 'L0_ffn_gup_lora_A': _L0_ffn_in['gup_lora_A'], 'L0_ffn_gup_lora_B': _L0_ffn_in['gup_lora_B'], 'L0_ffn_down_lora_A': _L0_ffn_in['down_lora_A'], 'L0_ffn_down_lora_B': _L0_ffn_in['down_lora_B'], 'L1_cond_Wq': _L1_cond_in['Wq'], 'L1_cond_Wk': _L1_cond_in['Wk'], 'L1_cond_Wv': _L1_cond_in['Wv'], 'L1_cond_Wo': _L1_cond_in['Wo'], 'L1_cond_q_norm_scale': _L1_cond_in['q_norm_scale'], 'L1_cond_k_norm_scale': _L1_cond_in['k_norm_scale'], 'L1_cond_k_blocks': _L1_cond_in['k_blocks'], 'L1_cond_v_blocks': _L1_cond_in['v_blocks'], 'L1_ffn_w_router': _L1_ffn_in['w_router'], 'L1_ffn_w_fc': _L1_ffn_in['w_fc'], 'L1_ffn_w_proj': _L1_ffn_in['w_proj']}

def reference(x, itok_B_1_198, itok_Bx257_0_4111, itok_B_37_3939, L0_cond_weights, L0_ffn_gate_weight, L0_ffn_gate_lora_A, L0_ffn_gate_lora_B, L0_ffn_gate_up_proj, L0_ffn_down_proj, L0_ffn_gup_lora_A, L0_ffn_gup_lora_B, L0_ffn_down_lora_A, L0_ffn_down_lora_B, L1_cond_Wq, L1_cond_Wk, L1_cond_Wv, L1_cond_Wo, L1_cond_q_norm_scale, L1_cond_k_norm_scale, L1_cond_k_blocks, L1_cond_v_blocks, L1_ffn_w_router, L1_ffn_w_fc, L1_ffn_w_proj):
    import jax
    import jax.numpy as jnp

    def _L0_cond_ref(x, conditions, weights):
        import jax, jax.numpy as jnp
        import numpy as np
        B, C, T = (128, 32, 256)
        S, D = (200, 32)
        w = weights[conditions]
        return jnp.einsum('bct,bcd->bdt', x, w)

    def _L0_ffn_ref(x, gate_weight, gate_lora_A, gate_lora_B, gate_up_proj, down_proj, gup_lora_A, gup_lora_B, down_lora_A, down_lora_B):
        import jax, jax.numpy as jnp
        import numpy as np
        TOP_K = 2
        SCALING = 2.0
        B, S, H = x.shape
        xf = x.reshape(-1, H)
        gate_delta = SCALING * (gate_lora_B @ gate_lora_A)
        router_logits = xf @ gate_weight.T + xf @ gate_delta.T
        probs = jax.nn.softmax(router_logits.astype(jnp.float32), axis=-1)
        routing_weights, selected = jax.lax.top_k(probs, TOP_K)
        routing_weights = routing_weights / routing_weights.sum(-1, keepdims=True)
        routing_weights = routing_weights.astype(xf.dtype)
        gup = jnp.einsum('th,eho->teo', xf, gate_up_proj)
        gup = gup + SCALING * jnp.einsum('ter,eor->teo', jnp.einsum('th,erh->ter', xf, gup_lora_A), gup_lora_B)
        gates, h = jnp.split(gup, 2, axis=-1)
        h = jax.nn.silu(gates) * h
        out = jnp.einsum('tei,eih->teh', h, down_proj)
        out = out + SCALING * jnp.einsum('ter,ehr->teh', jnp.einsum('tei,eri->ter', h, down_lora_A), down_lora_B)
        out_sel = jnp.take_along_axis(out, selected[:, :, None], axis=1)
        y = jnp.einsum('tkh,tk->th', out_sel, routing_weights)
        return y.reshape(B, S, H)

    def _L1_cond_ref(x, Wq, Wk, Wv, Wo, q_norm_scale, k_norm_scale, k_blocks, v_blocks, block_tables, kv_lens):
        import jax, jax.numpy as jnp
        import numpy as np
        H, G, HD = (8, 4, 32)
        GSZ = H // G
        BLOCK = 16
        WINDOW = 128
        SCALE = 256.0 ** (-0.5)
        EPS = 1e-06
        THETA = 10000.0
        B, T, D = (16, 4, 256)
        NBLK = 257

        def _rms(x, scale):
            var = jnp.mean(x * x, axis=-1, keepdims=True)
            return x * jax.lax.rsqrt(var + EPS) * (1.0 + scale)

        def _rope(x, pos):
            half = HD // 2
            inv = 1.0 / THETA ** (jnp.arange(half, dtype=jnp.float32) / half)
            ang = pos[:, :, None].astype(jnp.float32) * inv
            cos = jnp.cos(ang)[:, None, :, :]
            sin = jnp.sin(ang)[:, None, :, :]
            x1, x2 = (x[..., :half], x[..., half:])
            return jnp.concatenate([x1 * cos - x2 * sin, x2 * cos + x1 * sin], axis=-1)
        Bx, Tx, _ = x.shape
        q = jnp.einsum('btd,od->bto', x, Wq).reshape(Bx, Tx, H, HD).transpose(0, 2, 1, 3)
        k = jnp.einsum('btd,od->bto', x, Wk).reshape(Bx, Tx, G, HD).transpose(0, 2, 1, 3)
        v = jnp.einsum('btd,od->bto', x, Wv).reshape(Bx, Tx, G, HD).transpose(0, 2, 1, 3)
        q = _rms(q, q_norm_scale)
        k = _rms(k, k_norm_scale)
        pos = kv_lens[:, None] + jnp.arange(Tx, dtype=jnp.int32)
        q = _rope(q, pos)
        k = _rope(k, pos)
        slot = pos // BLOCK
        off = pos % BLOCK
        blk = jnp.take_along_axis(block_tables, slot, axis=1)
        k_blocks = k_blocks.at[blk, :, off, :].set(k.transpose(0, 2, 1, 3))
        v_blocks = v_blocks.at[blk, :, off, :].set(v.transpose(0, 2, 1, 3))
        k_all = k_blocks[block_tables].transpose(0, 2, 1, 3, 4).reshape(Bx, G, -1, HD)
        v_all = v_blocks[block_tables].transpose(0, 2, 1, 3, 4).reshape(Bx, G, -1, HD)
        S = k_all.shape[2]
        qg = q.reshape(Bx, G, GSZ, Tx, HD)
        scores = jnp.einsum('bghtd,bgsd->bghts', qg, k_all) * SCALE
        kpos = jnp.arange(S, dtype=jnp.int32)
        allowed = (kpos[None, None, :] <= pos[:, :, None]) & (kpos[None, None, :] > pos[:, :, None] - WINDOW)
        scores = jnp.where(allowed[:, None, None, :, :], scores, -jnp.inf)
        p = jax.nn.softmax(scores, axis=-1)
        o = jnp.einsum('bghts,bgsd->bghtd', p, v_all).reshape(Bx, H, Tx, HD)
        o = o.transpose(0, 2, 1, 3).reshape(Bx, Tx, H * HD)
        return jnp.einsum('bto,do->btd', o, Wo)

    def _L1_ffn_ref(x, w_router, w_fc, w_proj):
        import jax, jax.numpy as jnp
        import numpy as np
        DIM = 256
        HIDDEN = 1024
        NUM_EXPERTS = 2
        BATCH, SEQ = (4, 128)
        bsz, seq, dim = x.shape
        num_experts = w_router.shape[0]
        x_flat = x.reshape(-1, dim)
        logits = x_flat @ w_router.T
        probs = jax.nn.softmax(logits, axis=-1)
        top_idx = jnp.argmax(probs, axis=-1)
        top_weight = jnp.take_along_axis(probs, top_idx[:, None], axis=1)[:, 0]
        h = jnp.einsum('nd,ehd->enh', x_flat, w_fc)
        a = jnp.square(jnp.where(h >= 0, h, 0.5 * h))
        expert_out = jnp.einsum('enh,edh->end', a, w_proj)
        mask = (top_idx[None, :] == jnp.arange(num_experts)[:, None]).astype(x.dtype)
        out = jnp.einsum('end,en->nd', expert_out, mask * top_weight[None, :])
        return out.reshape(bsz, seq, dim)
    x = x + _L0_ffn_ref(_L0_cond_ref(x, itok_B_1_198, L0_cond_weights), L0_ffn_gate_weight, L0_ffn_gate_lora_A, L0_ffn_gate_lora_B, L0_ffn_gate_up_proj, L0_ffn_down_proj, L0_ffn_gup_lora_A, L0_ffn_gup_lora_B, L0_ffn_down_lora_A, L0_ffn_down_lora_B)
    x = x + _L1_ffn_ref(_L1_cond_ref(x, L1_cond_Wq, L1_cond_Wk, L1_cond_Wv, L1_cond_Wo, L1_cond_q_norm_scale, L1_cond_k_norm_scale, L1_cond_k_blocks, L1_cond_v_blocks, itok_Bx257_0_4111, itok_B_37_3939), L1_ffn_w_router, L1_ffn_w_fc, L1_ffn_w_proj)
    return x

_drawn_inputs = setup_inputs


def setup_inputs(seed=0):
    import zlib

    import numpy as np

    out = dict(_drawn_inputs(seed))
    spreads = {}
    factors = {}
    for name, (base, spread) in spreads.items():
        noise = np.random.default_rng([zlib.crc32(name.encode()), seed]).standard_normal(out[name].shape)
        drawn = base * np.exp(spread * noise) if base else spread * noise
        out[name] = jnp.asarray(drawn.astype(out[name].dtype))
    for name, factor in factors.items():
        out[name] = (out[name] * factor).astype(out[name].dtype)
    return out
```

```python
from contextlib import ExitStack

import numpy as np

import concourse.bass as bass
from concourse import mybir
from concourse.alu_op_type import AluOpType as ALU

F32 = mybir.dt.float32
I32 = mybir.dt.int32
ACT = mybir.ActivationFunctionType
AX = mybir.AxisListType

P = 128
B, T, D = 128, 32, 256
NT = B * T // P
BT = P // T
E0, I0, R0 = 8, 128, 16
E1, H1 = 2, 1024
N0 = (2 * B * T + E0 * (P - 1)) // P + 1
N1 = (B * T + E1 * (P - 1)) // P
H, G, HD = 8, 4, 32
KW = G * HD
BLK, NBLK, NPHYS = 16, 257, 4112
WIN = 128
NR = 11
NE = 3
KR = NR * BLK // 2
NK = 2 * KR
NH = H + G
QK = NH * HD
SCALE = 256.0 ** -0.5
EPS = 1e-6
BIG = 65536.0
TWO_PI = 2 * np.pi
C1 = 6.28125
C2 = round((TWO_PI - C1) * 2 ** 20) / 2 ** 20
C3 = TWO_PI - C1 - C2


def constants():
    at, cols, n = {}, [], 0
    p = np.arange(P)

    def put(name, a):
        nonlocal n
        a = np.broadcast_to(np.asarray(a, np.float32), (P, np.shape(a)[-1]))
        at[name] = (n, n + a.shape[1])
        cols.append(a)
        n += a.shape[1]

    put("ident", np.eye(P))
    put("before", np.triu(np.ones((P, P)), 1))
    put("ones", np.ones((1, P)))
    put("rev8", 8.0 - np.arange(8))
    put("freq", (np.float32(1.0) / np.power(np.float32(10000.0), np.arange(16, dtype=np.float32) / np.float32(16))))
    key = (2 * np.arange(KR)[None, :] + np.arange(2)[:, None]).reshape(1, -1)
    put("keypos", key - (p % T)[:, None])
    put("entry", (NE * np.arange(B)[None, :] + np.arange(NE)[:, None] + 1).reshape(1, -1))
    put("slotno", np.arange(NBLK)[None, :])
    put("entry_of", NE * p[:, None] + np.arange(NE)[None, :] + 1)
    put("ahead", np.concatenate([np.arange(NE), np.arange(NR)])[None, :])
    put("row48", np.arange(NE * BLK)[None, :])
    put("off48", (np.arange(NE * BLK) % BLK)[None, :])
    put("pair", np.tile(np.arange(8), NR)[None, :])
    put("tokmod", (p % T)[:, None])
    put("tileno", np.arange(80)[None, :])
    put("eps", np.full((P, 1), EPS))
    return np.ascontiguousarray(np.concatenate(cols, 1)), at


class Chain:

    def __init__(self, eng, sem):
        self.eng, self.sem, self.base, self.n = eng, sem, 0, 0

    def link(self, ins):
        self.n += 1
        ins.then_inc(self.sem, 1)
        self.eng.wait_ge(self.sem, self.base + self.n)

    def enter(self, k, per_round):
        self.start = self.base + self.n
        self.base, self.n, self.per_round = self.start + k * per_round, 0, per_round

    def leave(self, rounds):
        assert self.n == self.per_round, (self.n, self.per_round)
        self.base, self.n = self.start + rounds * self.per_round, 0


class Step:

    def __init__(self, s, r, q, n, unroll, full):
        self.s, self.r, self.q, self.n, self.unroll, self.full = s, r, q, n, unroll, full

    def has(self, off):
        return self.full or 0 <= self.s + off < self.n

    def slot(self, off=0):
        return (self.q + off) % self.unroll

    def turn(self, off=0):
        return self.r + (self.q + off) // self.unroll


def skewed(eng, n, unroll, lead, lag, chain=None, per_round=0):
    rounds = (n - lead - lag) // unroll
    for s in range(-lead, lag):
        yield Step(s, s // unroll, s % unroll, n, unroll, False)
    with eng.Fori(0, rounds) as k:
        if chain:
            chain.enter(k, per_round)
        for u in range(lag, lag + unroll):
            yield Step(k * unroll + u, k + u // unroll, u % unroll, n, unroll, True)
        if chain:
            chain.leave(rounds)
    for s in range(lag + rounds * unroll, n + lag):
        yield Step(s, s // unroll, s % unroll, n, unroll, False)


def wait(eng, sem, value):
    if isinstance(value, int):
        if value <= 0:
            return
    else:
        assert value.min_val >= 1, value.min_val
    eng.wait_ge(sem, value)


def col(ap, i, n=1):
    return ap[:, bass.ds(i, n)]


def build(nc, at, x, kv_lens, table, cond, consts, cond_w, gate_t, gate_a, gate_bt, gup, down, gup_a, gup_bt,
          down_a, down_bt, wqkv, wo, norm_scale, cache, router1, fc, proj, out):
    with ExitStack() as ctx:
        def sb(name, shape, dt=F32):
            return ctx.enter_context(nc.sbuf_tensor(name, shape, dt))

        def dram(name, shape):
            return nc.dram_tensor(name, shape, F32, kind="Internal").ap()

        def sem(name):
            return ctx.enter_context(nc.semaphore(name))

        def sems(name, n):
            return [sem(f"{name}{i}") for i in range(n)]

        bank = [ctx.enter_context(nc.psum_tensor(f"bank{i}", [P, 512], F32)) for i in range(8)]

        cw_dram = dram("cond_w_by_batch", [B * T, T])
        slots0 = dram("slots0_in", [N0 * P, D])
        slots0_out = dram("slots0_out", [N0 * P, D])
        x1_dram = dram("x1_rows", [B * T, D])
        copies = dram("written_blocks", [NE * B * BLK, 2 * KW])
        slots1 = dram("slots1_in", [N1 * P, D])
        slots1_out = dram("slots1_out", [N1 * P, D])

        cst = sb("cst", [P, consts.shape[1]])
        rows = sb("rows", [P, NT * D])
        qt = sb("qt", [P, NT * 2 * P])
        experts = sb("experts", [P, 8192])
        kvring = sb("kvring", [KR, 8 * 4 * KW])
        work = sb("work", [P, 10240])
        wqkv_sb = sb("wqkv_sb", [P, 2 * 512])
        wo_sb = sb("wo_sb", [P, 2 * D])
        nscale = sb("nscale", [P, QK])
        wr1 = sb("wr1", [P, E1 * D])
        gate_sb = sb("gate_sb", [P, 2 * E0])
        gate_a_sb = sb("gate_a_sb", [R0, D])
        gate_bt_sb = sb("gate_bt_sb", [R0, E0])
        cosine = sb("cosine", [P, NT * 16])
        sine = sb("sine", [P, NT * 16])
        kv_i = sb("kv_i", [P, 1], I32)
        cond_i = sb("cond_i", [P, 1], I32)
        table_i = sb("table_i", [P, NBLK], I32)
        small_i = sb("small_i", [P, 16], I32)
        small = sb("small", [P, 96])
        index_work = sb("index_work", [P, 640])
        guard = sb("guard", [P, 1])
        angle_i = sb("angle_i", [P, NT * 16], I32)
        entry_i = sb("entry_i", [P, NE], I32)
        dest_i = sb("dest_i", [P, NT], I32)
        read_i = sb("read_i", [KR, 2 * B], I32)
        delta = sb("delta", [P, B])
        logit0 = sb("logit0", [P, NT * E0])
        logit1 = sb("logit1", [P, NT * E1])
        route = sb("route", [P, 9 * 256])
        slot_i = sb("slot_i", [P, 3 * NT], I32)
        weight = sb("weight", [P, 3 * NT])
        tile_expert = sb("tile_expert", [P, 80])
        te0 = sb("te0", [P, 80], I32)
        te1 = sb("te1", [P, 80], I32)

        def c(name):
            a, b = at[name]
            return cst[:, a:b]

        ident = c("ident")

        s_const, s_int, s_lora, s_exp0, s_w, s_exp1 = (sem(n) for n in (
            "const_in", "ints_in", "lora_in", "experts0_in", "weights_in", "experts1_in"))
        s_cwg, s_cww, s_zero, s_zw = sem("condw_gathered"), sem("condw_written"), sem("zeroed"), sem("zeros_written")
        s_dv, s_ac = sem("dve_chain"), sem("act_chain")
        s_diag, s_er, s_cmp, s_cnt, s_turn, s_turned, s_idx = (sem(n) for n in (
            "diag_ready", "entry_rows_ready", "entry_compare_ready", "later_writers_counted", "turn_ready",
            "turned", "indices_ready"))
        s_blk, s_gate, s_gatec, s_ang, s_rope = (sem(n) for n in (
            "entry_blocks_ready", "gate_delta_ready", "gate_folded", "angles_ready", "rope_ready"))
        s_stg, s_stw = sem("block_staged"), sem("blocks_copied")
        s_fold, s_folded, s_scratch = sem("lora_product_ready"), sem("lora_folded"), sem("setup_scratch_free")

        block = ctx.enter_context(nc.Block())

        xt = [work[:, k * 256:k * 256 + 256] for k in range(4)]
        bd = [work[:, 1024 + k * 128:1152 + k * 128] for k in range(4)]
        yt = [work[:, 1536 + k * 256:1792 + k * 256] for k in range(4)]
        scratch = work[:, 2560:10240]
        s1_in = sems("x_and_condw_in", 4)
        s1_bd0, s1_y, s1_ytc, s1_yc, s1_lg, s1_lgc = (sem(n) for n in (
            "blockdiag_zeroed", "y_ready", "y_turned_copied", "y_copied", "logits_ready", "logits_copied"))
        s_oh, s_rank, s_slot, s_m, s_me = (sem(n) for n in (
            "onehot_ready", "ranks_ready", "slots_ready", "margin_ready", "margin_exp_ready"))
        s_sc0, s_sc1 = sem("rows_scattered0"), sem("rows_scattered1")
        xs = [work[:, k * 256:k * 256 + 256] for k in range(4)]
        xst = [work[:, 1024 + k * 256:1280 + k * 256] for k in range(2)]
        sg = [work[:, 1536 + k * 128:1664 + k * 128] for k in range(2)]
        ha = [work[:, 1792 + k * 128:1920 + k * 128] for k in range(2)]
        hat = [work[:, 2048 + k * 128:2176 + k * 128] for k in range(2)]
        os_ = [work[:, 2304 + k * 256:2560 + k * 256] for k in range(4)]
        s2_in, s2_out = sems("slot_tile_in", 4), sems("slot_tile_stored", 4)
        s2_t, s2_tc, s2_g, s2_sg, s2_a, s2_ta, s2_tac, s2_d, s2_dc = (sem("l0_" + n) for n in (
            "turned", "turned_copied", "gate_up", "silu", "hidden", "hidden_turned", "hidden_turned_copied",
            "down", "down_copied"))
        og = [[work[:, (2 * k + j) * 256:(2 * k + j) * 256 + 256] for j in range(2)] for k in range(4)]
        x1s = [work[:, 2048 + k * 256:2304 + k * 256] for k in range(4)]
        xr = [work[:, 3072 + k * 256:3328 + k * 256] for k in range(4)]
        qkv = [work[:, 4096 + k * 512:4608 + k * 512] for k in range(4)]
        x1t = [work[:, 6144 + k * 256:6400 + k * 256] for k in range(2)]
        sq = [work[:, 6656 + k * 384:7040 + k * 384] for k in range(2)]
        xn, xg, rc, rs = (work[:, 7424 + k * 384:7808 + k * 384] for k in range(4))
        x1a = work[:, 8960:9216]
        ms, sd, rinv = ([work[:, 9216 + k * 32 + j * 16:9228 + k * 32 + j * 16] for j in range(2)] for k in range(3))
        s3_og, s3_x, s3_st, s3_sc = sems("experts_out_in", 4), sems("x_in", 4), sems("x1_stored", 4), sems("kv_scattered", 4)
        s3_c, s3_t, s3_tc, s3_q, s3_sq, s3_v, s3_ms, s3_sd, s3_xn, s3_qk, s3_tq, s3_tqc = (sem("qkv_" + n) for n in (
            "combined", "turned", "turned_copied", "projected", "squared", "v_copied", "mean_square", "root",
            "normed", "roped", "q_turned", "q_turned_copied"))
        kv = [kvring[:, k * 512:k * 512 + 512] for k in range(8)]
        qbd = [work[:, k * 1024:k * 1024 + 1024] for k in range(2)]
        kt = [work[:, 2048 + k * 176:2224 + k * 176] for k in range(2)]
        dist = [work[:, 2400 + k * 176:2576 + k * 176] for k in range(2)]
        pen = [work[:, 2752 + k * 176:2928 + k * 176] for k in range(2)]
        sc = [work[:, 3104 + k * 352:3456 + k * 352] for k in range(2)]
        pr = [work[:, 3808 + k * 352:4160 + k * 352] for k in range(2)]
        pn = [work[:, 4512 + k * 352:4864 + k * 352] for k in range(2)]
        pt = [work[0:KR, 5216 + k * 512:5728 + k * 512] for k in range(2)]
        ot = [work[:, 6240 + k * 256:6496 + k * 256] for k in range(2)]
        mx, ng, sm, ri = ([work[:, 6752 + k * 8 + j * 4:6754 + k * 8 + j * 4] for j in range(2)] for k in range(4))
        junk = [work[:, 6784 + k * 256:7040 + k * 256] for k in range(2)]
        s4_in = sems("cache_rows_in", 8)
        (s4_z, s4_qbd, s4_kt, s4_ktc, s4_s, s4_di, s4_pen, s4_ttr, s4_ng, s4_ex, s4_ri, s4_pn, s4_tp, s4_tpc, s4_pv,
         s4_oc, s4_w, s4_wc, s4_lg) = (sem("att_" + n) for n in (
             "q_zeroed", "q_spread", "k_turned", "k_turned_copied", "scores", "distance", "penalty", "masked",
             "negmax", "exp", "recip", "probs", "probs_turned", "probs_turned_copied", "pv", "o_copied", "projected",
             "projected_copied", "logits"))
        ys = [work[:, k * 256:k * 256 + 256] for k in range(4)]
        yst = [work[:, 1024 + k * 256:1280 + k * 256] for k in range(2)]
        half = [work[:, 1536 + k * 512:2048 + k * 512] for k in range(2)]
        lk = [work[:, 2560 + k * 512:3072 + k * 512] for k in range(2)]
        av = [work[:, 3584 + k * 512:4096 + k * 512] for k in range(2)]
        avt = [work[:, 4608 + k * 512:5120 + k * 512] for k in range(2)]
        zs = [work[:, 5632 + k * 256:5888 + k * 256] for k in range(4)]
        s6_in, s6_out = sems("slot1_tile_in", 2), sems("slot1_tile_stored", 2)
        s6_t, s6_tc, s6_f, s6_h, s6_l, s6_a, s6_ta, s6_tac, s6_p, s6_pc = (sem("l1_" + n) for n in (
            "turned", "turned_copied", "fc", "halved", "leaky", "squared", "hidden_turned", "hidden_turned_copied",
            "proj", "proj_copied"))
        zg = [work[:, k * 256:k * 256 + 256] for k in range(4)]
        x1r = [work[:, 1024 + k * 256:1280 + k * 256] for k in range(4)]
        res = [work[:, 2048 + k * 256:2304 + k * 256] for k in range(4)]
        s7_g, s7_x, s7_st, s7_r = sems("expert1_out_in", 4), sems("x1_in", 4), sems("result_stored", 4), sem("result_ready")

        gup_v = experts[:, 0:E0 * 512]
        down_v = experts[:, E0 * 512:E0 * 768]
        fc_v = experts[:, 0:E1 * 2048]
        proj_v = experts[:, E1 * 2048:E1 * 4096]
        lora_gup_a, lora_gup_b = qt[0:R0, 0:2048], qt[0:R0, 2048:4096]
        lora_down_a, lora_down_b = qt[0:R0, 4096:5120], qt[0:R0, 5120:7168]
        copies_blocks = copies.rearrange("(b k r) f -> k b (r f)", k=NE, r=BLK)
        copies_pairs = copies.rearrange("(n r) f -> n (r f)", r=2)
        cache_blocks = cache.rearrange("(n r) f -> n (r f)", r=BLK)
        cache_pairs = cache.rearrange("(n r) f -> n (r f)", r=2)
        block_buffer = experts[:, 0:4096]
        cw_buffer = rows[:, 0:T * T]

        diag = scratch[:, 5376:5888]
        later = scratch[:, 6272:6272 + NE * NE * B]
        covers = index_work[:, 256:304]
        dest_b, read_b = index_work[:, 320:448], index_work[:, 448:624]
        onehot0, onehot1 = route[:, 1024:1280], route[:, 1024:1024 + NT * E1]

        def stage3_drained(eng):
            eng.wait_ge(s3_tq, NT)
            for k in range(4):
                eng.wait_ge(s3_st[k], 16 * NT // 4)
                eng.wait_ge(s3_sc[k], 16 * NT // 4)

        @block.sync
        def _(sp):
            sp.dma_start(cst[:], consts).then_inc(s_const, 16)
            sp.dma_start(cond_i[:], cond).then_inc(s_int, 16)
            sp.dma_start(kv_i[:], kv_lens).then_inc(s_int, 16)
            sp.dma_start(table_i[:], table).then_inc(s_int, 16)
            sp.dma_start(gate_sb[:], gate_t).then_inc(s_w, 16)
            sp.dma_start(gate_a_sb[:], gate_a).then_inc(s_w, 16)
            sp.dma_start(gate_bt_sb[:], gate_bt).then_inc(s_w, 16)
            sp.wait_ge(s_cwg, 16)
            sp.dma_start(cw_dram.rearrange("(b c) d -> b (c d)", b=B), cw_buffer).then_inc(s_cww, 16)
            sp.wait_ge(s_cww, 16)
            sp.wait_ge(s1_bd0, 1)
            for st in skewed(sp, NT, 4, 0, 4):
                if not st.has(0):
                    continue
                wait(sp, s1_y, st.s - 3)
                sp.dma_start(xt[st.q], x[bass.ds(st.s * P, P), :]).then_inc(s1_in[st.q], 16)
                for j in range(BT):
                    sp.dma_start(bd[st.q][T * j:T * j + T, T * j:T * j + T],
                                 cw_dram[bass.ds(st.s * P + T * j, T), :]).then_inc(s1_in[st.q], 16)
            sp.wait_ge(s_sc0, 16 * 2 * NT)
            for st in skewed(sp, N0, 4, 3, 5):
                if st.has(3):
                    wait(sp, s2_t, st.s)
                    sp.dma_start(xs[st.slot(3)], slots0[bass.ds((st.s + 3) * P, P), :]).then_inc(s2_in[st.slot(3)], 16)
                if st.has(-1):
                    sp.wait_ge(s2_dc, st.s)
                    sp.dma_start(slots0_out[bass.ds((st.s - 1) * P, P), :], os_[st.slot(-1)]).then_inc(
                        s2_out[st.slot(-1)], 16)
            sp.wait_ge(s2_d, N0)
            sp.dma_start(fc_v, fc).then_inc(s_exp1, 16)
            sp.dma_start(proj_v, proj).then_inc(s_exp1, 16)
            for k in range(4):
                sp.wait_ge(s2_out[k], 16 * ((N0 + 3 - k) // 4))
            for st in skewed(sp, NT, 4, 3, 5):
                if st.has(3):
                    wait(sp, s3_c, st.s)
                    sp.dma_start(xr[st.slot(3)], x[bass.ds((st.s + 3) * P, P), :]).then_inc(s3_x[st.slot(3)], 16)
                if st.has(-1):
                    sp.wait_ge(s3_c, st.s)
                    sp.dma_start(x1_dram[bass.ds((st.s - 1) * P, P), :], x1s[st.slot(-1)]).then_inc(
                        s3_st[st.slot(-1)], 16)
            sp.wait_ge(s_sc1, 16 * NT)
            for st in skewed(sp, N1, 2, 1, 3):
                if st.has(1):
                    wait(sp, s6_t, st.s)
                    sp.dma_start(ys[st.slot(1)], slots1[bass.ds((st.s + 1) * P, P), :]).then_inc(s6_in[st.slot(1)], 16)
                if st.has(-1):
                    sp.wait_ge(s6_pc, st.s)
                    sp.dma_start(slots1_out[bass.ds((st.s - 1) * P, P), :], zs[st.slot(-1)]).then_inc(
                        s6_out[st.slot(-1)], 16)
            for k in range(4):
                sp.wait_ge(s3_st[k], 16 * NT // 4)
            for k in range(2):
                sp.wait_ge(s6_out[k], 16 * ((N1 + 1 - k) // 2))
            for st in skewed(sp, NT, 4, 3, 5):
                if st.has(3):
                    wait(sp, s7_r, st.s)
                    sp.dma_start(x1r[st.slot(3)], x1_dram[bass.ds((st.s + 3) * P, P), :]).then_inc(s7_x[st.slot(3)], 16)
                if st.has(-1):
                    sp.wait_ge(s7_r, st.s)
                    sp.dma_start(out[bass.ds((st.s - 1) * P, P), :], res[st.slot(-1)]).then_inc(s7_st[st.slot(-1)], 16)
            for k in range(4):
                sp.wait_ge(s7_st[k], 16 * NT // 4)

        @block.gpsimd
        def _(pool):
            def gather(dst, src, index, done, bound=None):
                kw = {} if bound is None else {"bounds_check": bound, "oob_is_err": False}
                pool.indirect_dma_start(dst, None, src, bass.IndirectOffsetOnAxis(ap=index, axis=0), **kw).then_inc(done, 16)

            def scatter(dst, src, index, done, bound=None):
                kw = {} if bound is None else {"bounds_check": bound, "oob_is_err": False}
                pool.indirect_dma_start(dst, bass.IndirectOffsetOnAxis(ap=index, axis=0), src, None, **kw).then_inc(done, 16)

            pool.wait_ge(s_int, 48)
            gather(cw_buffer, cond_w.rearrange("s c d -> s (c d)"), cond_i[:, 0:1], s_cwg)
            pool.wait_ge(s_blk, 1)
            for k in range(NE):
                if k:
                    pool.wait_ge(s_stw, 16 * k)
                gather(block_buffer, cache_blocks, entry_i[:, k:k + 1], s_stg)
                pool.wait_ge(s_stg, 16 * (k + 1))
                pool.dma_start(copies_blocks[k], block_buffer).then_inc(s_stw, 16)
            pool.wait_ge(s_stw, 16 * NE)
            pool.wait_ge(s_slot, 1)
            pool.wait_ge(s1_yc, NT)
            pool.wait_ge(s_zw, 32)
            for i in range(NT):
                for j in range(2):
                    scatter(slots0, rows[:, i * D:i * D + D], slot_i[:, j * NT + i:j * NT + i + 1], s_sc0)
            pool.wait_ge(s_idx, 1)
            for b in range(8):
                gather(kv[b], cache_pairs, read_i[:, b:b + 1], s4_in[b], NPHYS * 8 - 1)
            for k in range(4):
                pool.wait_ge(s2_out[k], 16 * ((N0 + 3 - k) // 4))
            for i in range(NT + 3):
                if i < NT:
                    wait(pool, s3_c, i - 3)
                    for j in range(2):
                        gather(og[i % 4][j], slots0_out, slot_i[:, j * NT + i:j * NT + i + 1], s3_og[i % 4])
                if i >= 3:
                    pool.wait_ge(s3_qk, i - 2)
                    pool.wait_ge(s3_v, i - 2)
                    scatter(copies, qkv[(i - 3) % 4][:, 2 * P:512], dest_i[:, i - 3:i - 2], s3_sc[(i - 3) % 4],
                            NE * B * BLK - 1)
            for k in range(4):
                pool.wait_ge(s3_sc[k], 16 * NT // 4)
            for b in range(B + 2):
                if 8 <= b < B:
                    pool.wait_ge(s4_pv, b - 7)
                    gather(kv[b % 8], cache_pairs, read_i[:, b:b + 1], s4_in[b % 8], NPHYS * 8 - 1)
                if b >= 2:
                    c0 = b - 2
                    pool.wait_ge(s4_in[c0 % 8], 32 * (c0 // 8) + 16)
                    gather(kv[c0 % 8], copies_pairs, read_i[:, B + c0:B + c0 + 1], s4_in[c0 % 8], NE * B * 8 - 1)
            pool.wait_ge(s_slot, 2)
            pool.wait_ge(s4_wc, NT)
            for i in range(NT):
                scatter(slots1, rows[:, i * D:i * D + D], slot_i[:, 2 * NT + i:2 * NT + i + 1], s_sc1)
            for k in range(2):
                pool.wait_ge(s6_out[k], 16 * ((N1 + 1 - k) // 2))
            for i in range(NT):
                wait(pool, s7_r, i - 3)
                gather(zg[i % 4], slots1_out, slot_i[:, 2 * NT + i:2 * NT + i + 1], s7_g[i % 4])

        @block.scalar
        def _(act):
            ch = Chain(act, s_ac)
            act.dma_start(wqkv_sb[:], wqkv).then_inc(s_w, 16)
            act.dma_start(wo_sb[:], wo).then_inc(s_w, 16)
            act.dma_start(nscale[:], norm_scale).then_inc(s_w, 16)
            act.dma_start(wr1[:], router1).then_inc(s_w, 16)
            act.dma_start(lora_gup_a, gup_a).then_inc(s_lora, 16)
            act.dma_start(lora_gup_b, gup_bt).then_inc(s_lora, 16)
            act.dma_start(lora_down_a, down_a).then_inc(s_lora, 16)
            act.dma_start(lora_down_b, down_bt).then_inc(s_lora, 16)
            act.wait_ge(s_zero, 1)
            zeros = scratch[:, 7424:7680]
            for dst in (slots0, slots1):
                n = dst.shape[0] // P
                act.dma_start(dst.rearrange("(n p) d -> p n d", p=P),
                              zeros[:, None, :].broadcast_to([P, n, D])).then_inc(s_zw, 16)
            act.wait_ge(s_ang, 1)
            act.activation(sine[:], sine[:], ACT.Sin).then_inc(s_rope, 1)
            act.activation(cosine[:], cosine[:], ACT.Sin).then_inc(s_rope, 1)
            act.wait_ge(s_stw, 16 * NE)
            act.dma_start(gup_v, gup).then_inc(s_exp0, 16)
            act.dma_start(down_v, down).then_inc(s_exp0, 16)
            act.wait_ge(s_cww, 16)
            for st in skewed(act, NT, 4, 0, 0):
                act.wait_ge(s1_y, st.s + 1)
                act.activation(col(rows, st.s * D, D), bank[2 + st.q % 2][:, 0:D], ACT.Copy).then_inc(s1_yc, 1)
            act.wait_ge(s_m, 1)
            act.activation(weight[:, NT:2 * NT], weight[:, NT:2 * NT], ACT.Exp).then_inc(s_me, 1)
            for st in skewed(act, N0, 4, 1, 2):
                if st.has(1):
                    act.wait_ge(s2_g, st.s + 2)
                    wait(act, s2_a, st.s)
                    act.activation(sg[st.slot(1) % 2], bank[2 + st.slot(1) % 2][:, 0:I0], ACT.Silu).then_inc(s2_sg, 1)
                if st.has(0):
                    act.wait_ge(s2_ta, st.s + 1)
                    wait(act, s2_d, st.s - 1)
                    act.activation(hat[st.q % 2], bank[4 + st.q % 2][:, 0:P], ACT.Copy).then_inc(s2_tac, 1)
            for st in skewed(act, NT, 4, 1, 4):
                if st.has(1):
                    act.wait_ge(s3_t, st.s + 2)
                    wait(act, s3_q, st.s)
                    act.activation(x1t[st.slot(1) % 2], bank[st.slot(1) % 2][:, 0:D], ACT.Copy).then_inc(s3_tc, 1)
                if st.has(0):
                    act.wait_ge(s3_q, st.s + 1)
                    wait(act, s3_ms, st.s - 1)
                    act.activation(sq[st.q % 2], bank[2 + st.q % 2][:, 0:QK], ACT.Square).then_inc(s3_sq, 1)
                    wait(act, s3_sc[st.q], 16 * st.turn())
                    act.activation(qkv[st.q][:, QK:512], bank[2 + st.q % 2][:, QK:512], ACT.Copy).then_inc(s3_v, 1)
                    act.wait_ge(s3_ms, st.s + 1)
                    wait(act, s3_xn, st.s - 1)
                    act.activation(sd[st.q % 2], ms[st.q % 2], ACT.Sqrt, bias=c("eps"), scale=1.0 / HD).then_inc(s3_sd, 1)
                if st.has(-1):
                    act.wait_ge(s3_tq, st.s)
                    act.activation(col(qt, (st.s - 1) * 2 * P, 2 * P), bank[4 + st.slot(-1) % 2][:, 0:2 * P],
                                   ACT.Copy).then_inc(s3_tqc, 1)
            stage3_drained(act)
            act.wait_ge(s_idx, 1)
            for st in skewed(act, B, 8, 4, 7):
                if st.q % 2 == 1 and st.has(-2):
                    tile = 2 * st.turn(-3) + st.slot(-3) // 4
                    pair = st.slot(-3) // 2 % 2
                    act.wait_ge(s4_pv, st.s - 1)
                    dst = ot[st.slot(-3) // 4].rearrange("p (h b t) -> p b h t", h=2, b=BT)
                    src = bank[6][:, :].rearrange("p (b g h t) -> p b g h t", b=2, g=G, h=2)
                    for g in range(G):
                        act.activation(dst[HD * g:HD * g + HD, 2 * pair:2 * pair + 2, :, :],
                                       src[HD * g:HD * g + HD, :, g, :, :], ACT.Copy).then_inc(s4_oc, 1)
                if st.has(3):
                    act.wait_ge(s4_kt, st.s + 4)
                    wait(act, s4_s, st.s + 2)
                    act.activation(kt[st.slot(3) % 2], bank[st.slot(3) % 2][:, 0:NK], ACT.Copy).then_inc(s4_ktc, 1)
                    wait(act, s4_pen, st.s + 2)
                    act.activation(dist[st.slot(3) % 2], c("keypos"), ACT.Abs, bias=col(delta, st.s + 3)).then_inc(s4_di, 1)
                if st.has(1):
                    act.wait_ge(s4_ng, st.s + 2)
                    wait(act, s4_pn, st.s)
                    for g in range(2):
                        act.activation(pr[st.slot(1) % 2][:, g * NK:g * NK + NK], sc[st.slot(1) % 2][:, g * NK:g * NK + NK],
                                       ACT.Exp, bias=ng[st.slot(1) % 2][:, g:g + 1], scale=SCALE,
                                       accum_out=sm[st.slot(1) % 2][:, g:g + 1]).then_inc(s4_ex, 1)
                if st.q % 4 == 2 and st.has(-6):
                    tile = 2 * st.turn(-6) + st.slot(-6) // 4
                    act.wait_ge(s4_w, tile + 1)
                    act.activation(col(rows, tile * D, D), bank[7][:, 0:D], ACT.Copy).then_inc(s4_wc, 1)
            act.wait_ge(s_m, 2)
            act.activation(weight[:, 2 * NT:3 * NT], weight[:, 2 * NT:3 * NT], ACT.Exp).then_inc(s_me, 1)
            for st in skewed(act, 2 * N1, 4, 3, 2):
                if st.q % 2 == 1 and st.has(3):
                    tile, t = 2 * st.turn(3) + st.slot(3) // 2, st.slot(3) // 2
                    act.wait_ge(s6_t, tile + 1)
                    wait(act, s6_f, 2 * tile - 2)
                    act.activation(yst[t], bank[7 * t][:, 0:D], ACT.Copy).then_inc(s6_tc, 1)
                if st.has(2):
                    h = st.s + 2
                    act.wait_ge(s6_f, h + 1)
                    wait(act, s6_l, h - 1)
                    act.activation(half[st.slot(2) % 2], bank[1 + st.slot(2) % 2][:, :], ACT.Copy, scale=0.5).then_inc(s6_h, 1)
                    act.wait_ge(s6_l, h + 1)
                    wait(act, s6_ta, h - 1)
                    act.activation(av[st.slot(2) % 2], lk[st.slot(2) % 2], ACT.Square).then_inc(s6_a, 1)

        @block.tensor
        def _(pe):
            pe.wait_ge(s_const, 16)
            pe.wait_ge(s_diag, 1)
            pe.matmul(bank[0][:, :], c("ones"), diag, start=True, stop=True).then_inc(s_er, 1)
            pe.wait_ge(s_w, 16 * 7)
            for h in range(2):
                mm = pe.matmul(bank[3][:, h * E0:h * E0 + E0], gate_a_sb[:, h * P:h * P + P], gate_bt_sb[:, :],
                               start=True, stop=True)
            mm.then_inc(s_gate, 1)
            pe.wait_ge(s_cmp, 1)
            for k in range(NE):
                for k2 in range(NE):
                    mm = pe.matmul(bank[1][:, BLK * k:BLK * k + BLK], later[:, k2 * NE * B + k * B:k2 * NE * B + k * B + B],
                                   covers[:, BLK * k2:BLK * k2 + BLK], start=(k2 == 0), stop=(k2 == NE - 1))
            mm.then_inc(s_cnt, 1)
            pe.wait_ge(s_turn, 1)
            pe.transpose(bank[2][:, 0:P], dest_b, ident)
            for w in range(2):
                pe.transpose(bank[2][0:KR, P + w * B:P + w * B + B], read_b[:, w * KR:w * KR + KR], ident)
            pe.matmul(bank[2][:, 3 * P:4 * P], c("ones"), diag[:, 0:P], start=True, stop=True).then_inc(s_turned, 1)
            pe.wait_ge(s_gatec, 1)
            pe.wait_ge(s_idx, 1)
            for st in skewed(pe, NT, 4, 1, 2):
                if st.has(1):
                    q = st.slot(1)
                    pe.wait_ge(s1_in[q], 80 * st.turn(1) + 80)
                    wait(pe, s1_yc, st.s)
                    for h in range(2):
                        pe.matmul(bank[q % 2][:, h * P:h * P + P], xt[q][:, h * P:h * P + P], bd[q], start=True, stop=True)
                    pe.matmul(bank[2 + q % 2][:, 0:D], bd[q], xt[q], start=True, stop=True).then_inc(s1_y, 1)
                if st.has(0):
                    pe.wait_ge(s1_ytc, st.s + 1)
                    wait(pe, s1_lgc, st.s - 1)
                    for h in range(2):
                        mm = pe.matmul(bank[4 + st.q % 2][:, 0:E0], yt[st.q][:, h * P:h * P + P],
                                       gate_sb[:, h * E0:h * E0 + E0], start=(h == 0), stop=(h == 1))
                    mm.then_inc(s1_lg, 1)

            def ranks(onehot, n, turn):
                pe.wait_ge(s_oh, turn)
                pe.matmul(bank[6][:, 0:n], c("before"), onehot, start=True, stop=True)
                pe.matmul(bank[7][:, 0:n], c("ones"), onehot, start=True, stop=True).then_inc(s_rank, 1)

            ranks(onehot0, NT * E0, 1)
            pe.wait_ge(s_lora, 64)
            pe.wait_ge(s1_yc, NT)
            for e in range(E0):
                wait(pe, s_folded, 2 * (e - 1))
                for h in range(2):
                    pe.matmul(bank[e % 2][:, h * 256:h * 256 + 256], lora_gup_a[:, e * D + h * P:e * D + h * P + P],
                              lora_gup_b[:, e * 256:e * 256 + 256], start=True, stop=True)
                pe.matmul(bank[2 + e % 2][:, 0:D], lora_down_a[:, e * I0:e * I0 + I0],
                          lora_down_b[:, e * D:e * D + D], start=True, stop=True).then_inc(s_fold, 1)
            pe.wait_ge(s_folded, 2 * E0)
            for st in skewed(pe, N0, 4, 2, 3):
                if st.has(2):
                    q = st.slot(2)
                    pe.wait_ge(s2_in[q], 16 * st.turn(2) + 16)
                    for h in range(2):
                        mm = pe.transpose(bank[q % 2][:, h * P:h * P + P], xs[q][:, h * P:h * P + P], ident)
                    mm.then_inc(s2_t, 1)
                if st.has(1):
                    q = st.slot(1) % 2
                    expert = pe.value_load(te0[0:1, bass.ds(st.s + 1, 1)], min_val=0, max_val=E0 - 1)
                    pe.wait_ge(s2_tc, st.s + 2)
                    for h in range(2):
                        mm = pe.matmul(bank[2 + q][:, 0:256], xst[q][:, h * P:h * P + P],
                                       experts[:, bass.ds(expert * 512 + h * 256, 256)], start=(h == 0), stop=(h == 1))
                    mm.then_inc(s2_g, 1)
                if st.has(-1):
                    q = st.slot(-1) % 2
                    expert = pe.value_load(te0[0:1, bass.ds(st.s - 1, 1)], min_val=0, max_val=E0 - 1)
                    pe.wait_ge(s2_tac, st.s)
                    wait(pe, s2_dc, st.s - 2)
                    pe.matmul(bank[6 + q][:, 0:D], hat[q], experts[:, bass.ds(expert * 256 + E0 * 512, 256)],
                              start=True, stop=True).then_inc(s2_d, 1)
                if st.has(0):
                    q = st.q % 2
                    pe.wait_ge(s2_a, st.s + 1)
                    pe.transpose(bank[4 + q][:, 0:P], ha[q], ident).then_inc(s2_ta, 1)
            for st in skewed(pe, NT, 4, 1, 4):
                if st.has(1):
                    q = st.slot(1)
                    pe.wait_ge(s3_c, st.s + 2)
                    for h in range(2):
                        mm = pe.transpose(bank[q % 2][:, h * P:h * P + P], x1s[q][:, h * P:h * P + P], ident)
                    mm.then_inc(s3_t, 1)
                if st.has(0):
                    q = st.q % 2
                    pe.wait_ge(s3_tc, st.s + 1)
                    wait(pe, s3_xn, st.s - 1)
                    for h in range(2):
                        mm = pe.matmul(bank[2 + q][:, :], x1t[q][:, h * P:h * P + P], wqkv_sb[:, h * 512:h * 512 + 512],
                                       start=(h == 0), stop=(h == 1))
                    mm.then_inc(s3_q, 1)
                if st.has(-1):
                    q = st.slot(-1)
                    pe.wait_ge(s3_qk, st.s)
                    wait(pe, s3_tqc, st.s - 2)
                    for h in range(2):
                        mm = pe.transpose(bank[4 + q % 2][:, h * P:h * P + P], qkv[q][:, h * P:h * P + P], ident)
                    mm.then_inc(s3_tq, 1)
            for st in skewed(pe, B, 8, 4, 7):
                if st.has(3):
                    q = st.slot(3)
                    pe.wait_ge(s4_in[q], 32 * st.turn(3) + 32)
                    if not st.full and st.s < -1:
                        pe.wait_ge(s3_tqc, NT)
                    for r in range(2):
                        mm = pe.transpose(bank[q % 2][:, r * KR:r * KR + KR], kv[q][:, r * 256:r * 256 + KW], ident[0:KR, 0:KR])
                    mm.then_inc(s4_kt, 1)
                if st.has(2):
                    q, tile = st.slot(2), 2 * st.turn(2) + st.slot(2) // 4
                    pe.wait_ge(s4_ktc, st.s + 3)
                    pe.wait_ge(s4_qbd, G * (tile + 1))
                    wait(pe, s4_ng, st.s + 1)
                    for g in range(2):
                        mm = pe.matmul(bank[2 + q % 2][:, g * NK:g * NK + NK],
                                       qbd[q // 4][:, (q % 4) * 256 + g * P:(q % 4) * 256 + g * P + P], kt[q % 2],
                                       start=True, stop=True)
                    mm.then_inc(s4_s, 1)
                if st.has(-1):
                    q = st.slot(-1)
                    pe.wait_ge(s4_tpc, st.s)
                    if q % 2 == 0:
                        wait(pe, s4_oc, 2 * (st.s - 1))
                    for r in range(2):
                        mm = pe.matmul(bank[6][:, (q % 2) * 256:(q % 2) * 256 + 256], kv[q][:, r * 256 + KW:r * 256 + 2 * KW],
                                       pt[q % 2][:, r * 256:r * 256 + 256], start=(r == 0), stop=(r == 1))
                    mm.then_inc(s4_pv, 1)
                if st.has(0):
                    q = st.q
                    pe.wait_ge(s4_pn, st.s + 1)
                    for r in range(2):
                        for g in range(2):
                            mm = pe.transpose(bank[4 + q % 2][0:KR, (2 * r + g) * P:(2 * r + g) * P + P],
                                              pn[q % 2][:, g * NK + r * KR:g * NK + r * KR + KR], ident)
                    mm.then_inc(s4_tp, 1)
                if st.q % 4 == 2 and st.has(-6):
                    tile, t = 2 * st.turn(-6) + st.slot(-6) // 4, st.slot(-6) // 4
                    pe.wait_ge(s4_oc, 2 * G * (tile + 1))
                    wait(pe, s4_wc, tile)
                    for h in range(2):
                        mm = pe.matmul(bank[7][:, 0:D], ot[t][:, h * P:h * P + P], wo_sb[:, h * D:h * D + D],
                                       start=(h == 0), stop=(h == 1))
                    mm.then_inc(s4_w, 1)
            ranks(onehot1, NT * E1, 2)
            pe.wait_ge(s_exp1, 32)
            pe.wait_ge(s_slot, 2)
            for st in skewed(pe, 2 * N1, 4, 3, 4):
                if st.q % 2 == 1 and st.has(3):
                    t = st.slot(3) // 2
                    pe.wait_ge(s6_in[t], 16 * st.turn(3) + 16)
                    for h in range(2):
                        mm = pe.transpose(bank[7 * t][:, h * P:h * P + P], ys[t][:, h * P:h * P + P], ident)
                    mm.then_inc(s6_t, 1)
                if st.has(2):
                    n, t, tile = st.slot(2) % 2, st.slot(2) // 2, 2 * st.turn(2) + st.slot(2) // 2
                    expert = pe.value_load(te1[0:1, bass.ds(tile, 1)], min_val=0, max_val=E1 - 1)
                    pe.wait_ge(s6_tc, tile + 1)
                    for h in range(2):
                        mm = pe.matmul(bank[1 + n][:, :], yst[t][:, h * P:h * P + P],
                                       experts[:, bass.ds(expert * 2048 + h * H1 + n * 512, 512)],
                                       start=(h == 0), stop=(h == 1))
                    mm.then_inc(s6_f, 1)
                if st.has(0):
                    n, t, tile = st.q % 2, st.q // 2, 2 * st.turn() + st.q // 2
                    expert = pe.value_load(te1[0:1, bass.ds(tile, 1)], min_val=0, max_val=E1 - 1)
                    pe.wait_ge(s6_tac, st.s + 1)
                    if n == 0:
                        wait(pe, s6_pc, tile - 1)
                    for k in range(4):
                        mm = pe.matmul(bank[5 + t][:, 0:D], avt[n][:, k * P:k * P + P],
                                       experts[:, bass.ds(expert * 2048 + E1 * 2048 + (4 * n + k) * D, D)],
                                       start=(n == 0 and k == 0), stop=(n == 1 and k == 3))
                    mm.then_inc(s6_p, 1)
                if st.has(1):
                    n = st.slot(1) % 2
                    pe.wait_ge(s6_a, st.s + 2)
                    for k in range(4):
                        mm = pe.transpose(bank[3 + n][:, k * P:k * P + P], av[n][:, k * P:k * P + P], ident)
                    mm.then_inc(s6_ta, 1)

        @block.vector
        def _(dve):
            ch = Chain(dve, s_dv)
            link = ch.link
            dve.memset(work[:, 1024:1536], 0.0).then_inc(s1_bd0, 1)
            dve.memset(scratch[:, 7424:7680], 0.0).then_inc(s_zero, 1)
            dve.wait_ge(s_const, 16)
            dve.wait_ge(s_int, 48)

            length, first, last_off = small[:, 0:1], small[:, 2:3], small[:, 4:5]
            start = small[:, 5:6]
            slots, blocks, owner = small[:, 8:22], small[:, 24:38], small[:, 40:54]
            link(dve.tensor_copy(length, kv_i[:]))
            link(dve.tensor_scalar(small[:, 1:2], length, 1.0, None, ALU.add))
            link(dve.tensor_copy(small_i[:, 0:1], small[:, 1:2]))
            dve.tensor_scalar(small_i[:, 1:2], kv_i[:], 4, None, ALU.arith_shift_right)
            dve.tensor_scalar(small_i[:, 2:3], small_i[:, 0:1], 4, None, ALU.arith_shift_right)
            link(dve.tensor_scalar(small_i[:, 3:4], kv_i[:], BLK - 1, None, ALU.bitwise_and))
            link(dve.tensor_copy(small[:, 2:5], small_i[:, 1:4]))
            link(dve.tensor_scalar(start, small[:, 3:4], -float(WIN // BLK), 0.0, ALU.add, ALU.max))
            link(dve.tensor_scalar(start, start, float(NBLK - NR), None, ALU.min))
            dve.tensor_scalar(slots[:, 0:NE], c("ahead")[:, 0:NE], first, float(NBLK - 1), ALU.add, ALU.min)
            dve.tensor_scalar(slots[:, NE:NE + NR], c("ahead")[:, NE:NE + NR], start, None, ALU.add)
            tablef = scratch[:, 0:NBLK]
            link(dve.tensor_copy(tablef, table_i[:]))
            for k in range(NE + NR):
                ins = dve.scalar_tensor_tensor(out=scratch[:, NBLK * (k + 1):NBLK * (k + 2)], in0=c("slotno"),
                                               scalar=slots[:, k:k + 1], in1=tablef, op0=ALU.is_equal, op1=ALU.mult,
                                               accum_out=blocks[:, k:k + 1])
            link(ins)
            dve.tensor_copy(entry_i[:], blocks[:, 0:NE]).then_inc(s_blk, 1)
            for k in range(NE):
                dve.tensor_scalar(diag[:, k * B:k * B + B], ident, blocks[:, k:k + 1], None, ALU.mult)
            dve.tensor_scalar(diag[:, NE * B:], ident, length, None, ALU.mult).then_inc(s_diag, 1)
            dve.wait_ge(s_er, 1)
            entry_rows = scratch[:, 5888:6272]
            tokpos = index_work[:, 0:NT]
            dve.tensor_copy(entry_rows, bank[0][:, 0:NE * B])
            for j in range(BT):
                p0 = T * j
                ins = dve.tensor_scalar(tokpos[p0:p0 + T, :],
                                        bank[0][p0:p0 + T, NE * B:].rearrange("p (i j) -> p j i", j=BT)[:, j, :],
                                        c("tokmod")[p0:p0 + T, :], None, ALU.add)
            link(ins)
            for k in range(NE):
                ins = dve.tensor_scalar(later[:, k * NE * B:(k + 1) * NE * B], c("entry"), c("entry_of")[:, k:k + 1], None, ALU.is_lt)
            dve.tensor_scalar(index_work[:, 32:80], c("row48"), last_off, None, ALU.is_ge)
            link(dve.tensor_scalar(small[:, 6:7], last_off, float(T), None, ALU.add))
            for k in range(NE):
                dve.scalar_tensor_tensor(out=later[:, k * NE * B:(k + 1) * NE * B], in0=entry_rows, scalar=blocks[:, k:k + 1],
                                         in1=later[:, k * NE * B:(k + 1) * NE * B], op0=ALU.is_equal, op1=ALU.mult)
            dve.scalar_tensor_tensor(out=covers, in0=c("row48"), scalar=small[:, 6:7], in1=index_work[:, 32:80],
                                     op0=ALU.is_lt, op1=ALU.mult).then_inc(s_cmp, 1)
            match = scratch[:, 0:14 * NE * B]
            for k in range(NE + NR):
                ins = dve.scalar_tensor_tensor(out=match[:, k * NE * B:(k + 1) * NE * B], in0=entry_rows,
                                               scalar=blocks[:, k:k + 1], in1=c("entry"), op0=ALU.is_equal, op1=ALU.mult)
            link(ins)
            link(dve.tensor_reduce(owner, match.rearrange("p (k e) -> p k e", k=NE + NR), AX.X, ALU.max))
            dve.wait_ge(s_cnt, 1)
            row = index_work[:, 128:176]
            dve.tensor_scalar(index_work[:, 32:80], bank[1][:, 0:NE * BLK], 0.5, None, ALU.is_lt)
            dve.tensor_scalar(index_work[:, 176:192], c("row48")[:, 0:BLK], last_off, None, ALU.is_equal)
            link(dve.tensor_scalar(small[:, 56:59], owner[:, 0:NE], float(BLK), 1.0 - BLK, ALU.mult, ALU.add))
            for k in range(NE):
                ins = dve.tensor_scalar(row[:, BLK * k:BLK * k + BLK], c("off48")[:, BLK * k:BLK * k + BLK],
                                        small[:, 56 + k:57 + k], None, ALU.add)
            link(ins)
            link(dve.tensor_tensor(row, row, index_work[:, 32:80], ALU.mult))
            acc = [index_work[:, 192:224], index_work[:, 224:256]]
            link(dve.memset(acc[0], 0.0))
            for r in range(BLK):
                link(dve.scalar_tensor_tensor(out=acc[(r + 1) % 2], in0=row[:, r:r + T], scalar=index_work[:, 176 + r:177 + r],
                                              in1=acc[r % 2], op0=ALU.mult, op1=ALU.add))
            dve.tensor_copy(dest_b.rearrange("p (j t) -> p j t", j=BT), acc[0][:, None, :].broadcast_to([P, BT, T]))
            dve.tensor_scalar(small[:, 60:71], owner[:, NE:], 0.5, BIG, ALU.is_gt, ALU.mult)
            link(dve.tensor_scalar(small[:, 72:83], owner[:, NE:], 0.5, BIG, ALU.is_lt, ALU.mult))
            dve.scalar_tensor_tensor(out=small[:, 60:71], in0=blocks[:, NE:], scalar=8.0, in1=small[:, 60:71],
                                     op0=ALU.mult, op1=ALU.add)
            link(dve.scalar_tensor_tensor(out=small[:, 72:83], in0=owner[:, NE:], scalar=8.0, in1=small[:, 72:83],
                                          op0=ALU.mult, op1=ALU.add))
            link(dve.tensor_scalar(small[:, 72:83], small[:, 72:83], -8.0, None, ALU.add))
            for w in range(2):
                dve.tensor_tensor(read_b[:, w * KR:w * KR + KR].rearrange("p (k o) -> p k o", k=NR),
                                  small[:, 60 + 12 * w:71 + 12 * w][:, :, None].broadcast_to([P, NR, 8]),
                                  c("pair").rearrange("p (k o) -> p k o", k=NR), ALU.add)
            link(dve.scalar_tensor_tensor(out=small[:, 7:8], in0=start, scalar=float(BLK), in1=length,
                                          op0=ALU.mult, op1=ALU.subtract))
            link(dve.tensor_scalar(small[:, 7:8], small[:, 7:8], (WIN - 1) / 2, None, ALU.add))
            dve.tensor_scalar(diag[:, 0:P], ident, small[:, 7:8], None, ALU.mult).then_inc(s_turn, 1)
            dve.wait_ge(s_turned, 1)
            tokrow = index_work[:, 80:112]
            for j in range(BT):
                p0 = T * j
                ins = dve.tensor_copy(tokrow[p0:p0 + T, :],
                                      bank[2][p0:p0 + T, 0:P].rearrange("p (i j) -> p j i", j=BT)[:, j, :])
            link(ins)
            link(dve.tensor_scalar(acc[1], tokrow, 0.5, None, ALU.is_lt))
            link(dve.scalar_tensor_tensor(out=acc[0], in0=acc[1], scalar=BIG, in1=tokrow, op0=ALU.mult, op1=ALU.add))
            dve.tensor_scalar(dest_i[:], acc[0], -1.0, None, ALU.add)
            dve.tensor_copy(read_i[:], bank[2][0:KR, P:3 * P])
            dve.wait_ge(s_gate, 1)
            dve.scalar_tensor_tensor(out=gate_sb[:], in0=bank[3][:, 0:2 * E0], scalar=2.0, in1=gate_sb[:],
                                     op0=ALU.mult, op1=ALU.add).then_inc(s_gatec, 1)
            dve.tensor_copy(delta[:], bank[2][:, 3 * P:]).then_inc(s_idx, 1)

            ang, turns = route[:, 0:512], route[:, 512:1024]
            link(dve.tensor_tensor(ang.rearrange("p (i f) -> p i f", f=16), tokpos[:, :, None].broadcast_to([P, NT, 16]),
                                   c("freq")[:, None, :].broadcast_to([P, NT, 16]), ALU.mult))
            link(dve.tensor_scalar(turns, ang, 1.0 / TWO_PI, None, ALU.mult))
            link(dve.tensor_copy(angle_i[:], turns))
            link(dve.tensor_copy(turns, angle_i[:]))
            for part in (C1, C2, C3):
                link(dve.scalar_tensor_tensor(out=ang, in0=turns, scalar=-part, in1=ang, op0=ALU.mult, op1=ALU.add))
            link(dve.tensor_scalar(cosine[:], ang, float(np.pi / 2), None, ALU.add))
            link(dve.tensor_copy(sine[:], ang))
            for a in (sine, cosine):
                link(dve.tensor_scalar(turns, a[:], float(np.pi), -TWO_PI, ALU.is_gt, ALU.mult))
                link(dve.tensor_tensor(a[:], a[:], turns, ALU.add))
                link(dve.tensor_scalar(turns, a[:], float(-np.pi), TWO_PI, ALU.is_lt, ALU.mult))
                link(dve.tensor_tensor(a[:], a[:], turns, ALU.add))
                ins = dve.tensor_scalar(a[:], a[:], 3.1415925, -3.1415925, ALU.min, ALU.max)
                if a is sine:
                    link(ins)
            ins.then_inc(s_ang, 1)

            for st in skewed(dve, NT, 4, 1, 1):
                if st.has(1):
                    q = st.slot(1)
                    dve.wait_ge(s1_y, st.s + 2)
                    dve.tensor_copy(yt[q], bank[q % 2][:, 0:D]).then_inc(s1_ytc, 1)
                if st.has(0):
                    dve.wait_ge(s1_lg, st.s + 1)
                    dve.tensor_copy(col(logit0, st.s * E0, E0), bank[4 + st.q % 2][:, 0:E0]).then_inc(s1_lgc, 1)

            def by_expert(ap, n):
                return ap.rearrange("p (i e) -> p i e", e=n)

            def spread(ap, n):
                return ap[:, :, None].broadcast_to([P, NT, n])

            buf = [route[:, 256 * k:256 * k + 256] for k in range(9)]
            b_eq, b_first, b_rest, b_second, _, b_incl, b_slot, b_prod, b_small = buf
            rev = c("rev8")[:, None, :].broadcast_to([P, NT, E0])
            dve.wait_ge(s_rope, 2)
            dve.wait_ge(s1_lgc, NT)

            def best(logits, onehot, top):
                link(dve.tensor_reduce(top, by_expert(logits, E0), AX.X, ALU.max))
                link(dve.tensor_tensor(by_expert(b_eq, E0), by_expert(logits, E0), spread(top, E0), ALU.is_equal))
                link(dve.tensor_tensor(by_expert(b_eq, E0), by_expert(b_eq, E0), rev, ALU.mult))
                link(dve.tensor_reduce(b_small[:, 96:128], by_expert(b_eq, E0), AX.X, ALU.max))
                link(dve.tensor_tensor(by_expert(onehot, E0), rev, spread(b_small[:, 96:128], E0), ALU.is_equal))

            best(logit0[:], b_first, b_small[:, 0:32])
            link(dve.scalar_tensor_tensor(out=b_rest, in0=b_first, scalar=-1e30, in1=logit0[:], op0=ALU.mult, op1=ALU.add))
            best(b_rest, b_second, b_small[:, 32:64])
            dve.tensor_tensor(onehot0, b_first, b_second, ALU.add).then_inc(s_oh, 1)
            dve.tensor_tensor(weight[:, NT:2 * NT], b_small[:, 32:64], b_small[:, 0:32], ALU.subtract).then_inc(s_m, 1)

            def slots_of(n, turn, te_i):
                cnt, nt, end, beg = (b_small[:, 128 + 8 * k:128 + 8 * k + n] for k in range(4))
                dve.wait_ge(s_rank, turn)
                incl, total = by_expert(b_incl[:, 0:NT * n], n), by_expert(bank[7][:, 0:NT * n], n)
                for e in range(n):
                    ins = dve.tensor_tensor_scan(incl[:, :, e], c("ones")[:, 0:NT], total[:, :, e], 0.0, ALU.mult, ALU.add)
                link(ins)
                link(dve.tensor_scalar(cnt, incl[:, NT - 1, :], float(P - 1), None, ALU.add))
                link(dve.tensor_copy(small_i[:, 0:n], cnt))
                link(dve.tensor_scalar(small_i[:, 8:8 + n], small_i[:, 0:n], 7, None, ALU.arith_shift_right))
                link(dve.tensor_copy(nt, small_i[:, 8:8 + n]))
                link(dve.tensor_tensor_scan(end, c("ones")[:, 0:n], nt, 0.0, ALU.mult, ALU.add))
                link(dve.tensor_tensor(beg, end, nt, ALU.subtract))
                link(dve.tensor_scalar(beg, beg, float(P), None, ALU.mult))
                slot = by_expert(b_slot[:, 0:NT * n], n)
                link(dve.tensor_tensor(slot, incl, total, ALU.subtract))
                link(dve.tensor_tensor(b_slot[:, 0:NT * n], b_slot[:, 0:NT * n], bank[6][:, 0:NT * n], ALU.add))
                link(dve.tensor_tensor(slot, slot, beg[:, None, :].broadcast_to([P, NT, n]), ALU.add))
                link(dve.memset(tile_expert[:], 0.0))
                for e in range(n):
                    link(dve.scalar_tensor_tensor(out=tile_expert[:], in0=c("tileno"), scalar=end[:, e:e + 1],
                                                  in1=tile_expert[:], op0=ALU.is_ge, op1=ALU.add))
                link(dve.tensor_scalar(te_i[:], tile_expert[:], float(n - 1), None, ALU.min))

            def pick(onehot, n, dst):
                link(dve.tensor_tensor(b_prod[:, 0:NT * n], onehot, b_slot[:, 0:NT * n], ALU.mult))
                link(dve.tensor_reduce(b_small[:, 64:96], by_expert(b_prod[:, 0:NT * n], n), AX.X, ALU.add))
                return dve.tensor_copy(dst, b_small[:, 64:96])

            slots_of(E0, 1, te0)
            link(pick(b_first, E0, slot_i[:, 0:NT]))
            pick(b_second, E0, slot_i[:, NT:2 * NT]).then_inc(s_slot, 1)
            dve.wait_ge(s_me, 1)
            link(dve.tensor_scalar(weight[:, 0:NT], weight[:, NT:2 * NT], 1.0, None, ALU.add))
            link(dve.reciprocal(weight[:, 0:NT], weight[:, 0:NT]))
            link(dve.tensor_tensor(weight[:, NT:2 * NT], weight[:, NT:2 * NT], weight[:, 0:NT], ALU.mult))
            dve.wait_ge(s_exp0, 32)
            for e in range(E0):
                dve.wait_ge(s_fold, e + 1)
                dve.scalar_tensor_tensor(out=gup_v[:, e * 512:e * 512 + 512], in0=bank[e % 2][:, :], scalar=2.0,
                                         in1=gup_v[:, e * 512:e * 512 + 512], op0=ALU.mult, op1=ALU.add).then_inc(s_folded, 1)
                dve.scalar_tensor_tensor(out=down_v[:, e * 256:e * 256 + 256], in0=bank[2 + e % 2][:, 0:D], scalar=2.0,
                                         in1=down_v[:, e * 256:e * 256 + 256], op0=ALU.mult, op1=ALU.add).then_inc(s_folded, 1)

            for st in skewed(dve, N0, 4, 2, 5):
                if st.has(2):
                    q = st.slot(2) % 2
                    dve.wait_ge(s2_t, st.s + 3)
                    wait(dve, s2_g, st.s + 1)
                    dve.tensor_copy(xst[q], bank[q][:, 0:D]).then_inc(s2_tc, 1)
                if st.has(1):
                    q = st.slot(1) % 2
                    dve.wait_ge(s2_sg, st.s + 2)
                    wait(dve, s2_ta, st.s)
                    dve.tensor_tensor(ha[q], sg[q], bank[2 + q][:, I0:2 * I0], ALU.mult).then_inc(s2_a, 1)
                if st.has(-1):
                    q = st.slot(-1)
                    dve.wait_ge(s2_d, st.s)
                    wait(dve, s2_out[q], 16 * st.turn(-1))
                    dve.tensor_copy(os_[q], bank[6 + q % 2][:, 0:D]).then_inc(s2_dc, 1)

            dve.wait_ge(s_w, 16 * 7)
            link(dve.tensor_scalar(nscale[:], nscale[:], 1.0, None, ALU.add))
            for st in skewed(dve, NT, 4, 2, 4, ch, 24):
                if st.has(2):
                    q, tile = st.slot(2), st.s + 2
                    dve.wait_ge(s3_og[q], 32 * st.turn(2) + 32)
                    dve.wait_ge(s3_x[q], 16 * st.turn(2) + 16)
                    wait(dve, s3_c, tile)
                    link(dve.scalar_tensor_tensor(out=x1a, in0=og[q][0], scalar=col(weight, tile), in1=xr[q],
                                                  op0=ALU.mult, op1=ALU.add))
                    wait(dve, s3_t, st.s - 1)
                    wait(dve, s3_st[q], 16 * st.turn(2))
                    dve.scalar_tensor_tensor(out=x1s[q], in0=og[q][1], scalar=col(weight, tile + NT), in1=x1a,
                                             op0=ALU.mult, op1=ALU.add).then_inc(s3_c, 1)
                if st.has(0):
                    q = st.q % 2
                    dve.wait_ge(s3_sq, st.s + 1)
                    dve.tensor_reduce(ms[q], sq[q].rearrange("p (h d) -> p h d", h=NH), AX.X, ALU.add).then_inc(s3_ms, 1)
                    dve.wait_ge(s3_sd, st.s + 1)
                    dve.wait_ge(s3_v, st.s + 1)
                    link(dve.reciprocal(rinv[q], sd[q]))
                    heads = lambda ap: ap.rearrange("p (h d) -> p h d", h=NH)
                    dve.tensor_tensor(heads(xn), heads(bank[2 + q][:, 0:QK]), rinv[q][:, :, None].broadcast_to([P, NH, HD]),
                                      ALU.mult).then_inc(s3_xn, 1)
                    dve.wait_ge(s3_xn, st.s + 1)
                    link(dve.tensor_tensor(xg, xn, nscale[:], ALU.mult))
                    hv = lambda ap: ap.rearrange("p (h f) -> p h f", f=16)
                    for dst, tab in ((rc, cosine), (rs, sine)):
                        link(dve.tensor_tensor(hv(dst), hv(xg), col(tab, st.s * 16, 16)[:, None, :].broadcast_to([P, 2 * NH, 16]),
                                               ALU.mult))
                    wait(dve, s3_tq, st.s - 3)
                    wait(dve, s3_sc[st.q], 16 * st.turn())
                    lo, hi = (lambda ap: ap.rearrange("p (h w f) -> p h w f", h=NH, w=2)[:, :, 0, :],
                              lambda ap: ap.rearrange("p (h w f) -> p h w f", h=NH, w=2)[:, :, 1, :])
                    o = qkv[st.q][:, 0:QK]
                    link(dve.tensor_tensor(lo(o), lo(rc), hi(rs), ALU.subtract))
                    dve.tensor_tensor(hi(o), hi(rc), lo(rs), ALU.add).then_inc(s3_qk, 1)

            stage3_drained(dve)
            link(dve.memset(work[:, 0:2048], 0.0))
            dve.wait_ge(s3_tqc, NT)
            for st in skewed(dve, B, 8, 4, 7, ch, 10):
                if st.q % 4 == 0 and st.has(4):
                    tile, t = 2 * st.turn(4) + st.slot(4) // 4, st.slot(4) // 4
                    wait(dve, s4_s, st.s)
                    for g in range(G):
                        p0 = HD * g
                        src = qt[p0:p0 + HD, bass.ds(tile * 2 * P, 2 * P)].rearrange("p (h b t) -> p b h t", h=2, b=BT)
                        dst = qbd[t][p0:p0 + HD, :].rearrange("p (b g h t) -> p b g h t", b=BT, g=G, h=2)[:, :, g, :, :]
                        dve.tensor_copy(dst, src).then_inc(s4_qbd, 1)
                if st.has(2):
                    q = st.slot(2) % 2
                    dve.wait_ge(s4_di, st.s + 3)
                    dve.tensor_scalar(pen[q], dist[q], WIN / 2, -1e30, ALU.is_gt, ALU.mult).then_inc(s4_pen, 1)
                    wait(dve, s4_ex, 2 * (st.s + 1))
                    dve.wait_ge(s4_s, st.s + 3)
                    dve.wait_ge(s4_pen, st.s + 3)
                    dve.memset(guard[:], 0.0)
                    for g in range(2):
                        dve.tensor_tensor_reduce(sc[q][:, g * NK:g * NK + NK], bank[2 + q][:, g * NK:g * NK + NK], pen[q],
                                                 1.0, -3e38, ALU.add, ALU.max, mx[q][:, g:g + 1]).then_inc(s4_ttr, 1)
                    dve.wait_ge(s4_ttr, 2 * (st.s + 3))
                    dve.tensor_scalar(ng[q], mx[q], -SCALE, None, ALU.mult).then_inc(s4_ng, 1)
                if st.has(1):
                    q = st.slot(1) % 2
                    dve.wait_ge(s4_ex, 2 * (st.s + 2))
                    link(dve.reciprocal(ri[q], sm[q]))
                    wait(dve, s4_tp, st.s)
                    for g in range(2):
                        ins = dve.tensor_scalar(pn[q][:, g * NK:g * NK + NK], pr[q][:, g * NK:g * NK + NK], ri[q][:, g:g + 1],
                                                None, ALU.mult)
                    ins.then_inc(s4_pn, 1)
                if st.has(0):
                    q = st.q % 2
                    dve.wait_ge(s4_tp, st.s + 1)
                    wait(dve, s4_pv, st.s - 1)
                    dve.tensor_copy(pt[q], bank[4 + q][0:KR, :]).then_inc(s4_tpc, 1)
                if st.q % 4 == 3 and st.has(-7):
                    tile = 2 * st.turn(-7) + st.slot(-7) // 4
                    dve.wait_ge(s4_wc, tile + 1)
                    for e in range(E1):
                        ins = dve.scalar_tensor_tensor(out=junk[e], in0=col(rows, tile * D, D), scalar=1.0,
                                                       in1=wr1[:, e * D:e * D + D], op0=ALU.mult, op1=ALU.mult,
                                                       accum_out=col(logit1, tile * E1 + e))
                    link(ins)

            oh1 = by_expert(onehot1, E1)
            lg = by_expert(logit1[:], E1)
            margin = b_small[:, 0:32]
            link(dve.tensor_tensor(margin, lg[:, :, 1], lg[:, :, 0], ALU.subtract))
            dve.tensor_scalar(oh1[:, :, 0], margin, 0.0, None, ALU.is_le)
            dve.tensor_scalar(oh1[:, :, 1], margin, 0.0, None, ALU.is_gt).then_inc(s_oh, 1)
            link(dve.tensor_scalar(weight[:, 2 * NT:], margin, -1.0, None, ALU.mult))
            dve.tensor_tensor(weight[:, 2 * NT:], weight[:, 2 * NT:], margin, ALU.min).then_inc(s_m, 1)
            slots_of(E1, 2, te1)
            pick(onehot1, E1, slot_i[:, 2 * NT:]).then_inc(s_slot, 1)
            dve.wait_ge(s_me, 2)
            link(dve.tensor_scalar(weight[:, 2 * NT:], weight[:, 2 * NT:], 1.0, None, ALU.add))
            link(dve.reciprocal(weight[:, 2 * NT:], weight[:, 2 * NT:]))

            for st in skewed(dve, 2 * N1, 4, 3, 4):
                if st.has(2):
                    q = st.slot(2) % 2
                    dve.wait_ge(s6_h, st.s + 3)
                    wait(dve, s6_a, st.s + 1)
                    dve.tensor_tensor(lk[q], bank[1 + q][:, :], half[q], ALU.max).then_inc(s6_l, 1)
                if st.has(1):
                    q = st.slot(1) % 2
                    dve.wait_ge(s6_ta, st.s + 2)
                    wait(dve, s6_p, st.s)
                    dve.tensor_copy(avt[q], bank[3 + q][:, :]).then_inc(s6_tac, 1)
                if st.q % 2 == 1 and st.has(0):
                    t = st.q // 2
                    dve.wait_ge(s6_p, st.s + 1)
                    wait(dve, s6_out[t], 16 * st.turn())
                    dve.tensor_copy(zs[t], bank[5 + t][:, 0:D]).then_inc(s6_pc, 1)

            for st in skewed(dve, NT, 4, 0, 4):
                if not st.has(0):
                    continue
                dve.wait_ge(s7_g[st.q], 16 * st.turn() + 16)
                dve.wait_ge(s7_x[st.q], 16 * st.turn() + 16)
                wait(dve, s7_st[st.q], 16 * st.turn())
                dve.scalar_tensor_tensor(out=res[st.q], in0=zg[st.q], scalar=col(weight, st.s + 2 * NT), in1=x1r[st.q],
                                         op0=ALU.mult, op1=ALU.add).then_inc(s7_r, 1)


def kernel(**inputs):
    import concourse.bacc as bacc
    from concourse.bass_utils import run_bass_kernel_spmd as run

    a = {k: np.asarray(v) for k, v in inputs.items()}

    def halves(w):
        return w.reshape(-1, P, w.shape[-1]).transpose(1, 0, 2).reshape(P, -1)

    consts, at = constants()
    q_order = lambda w: w.reshape(G, 2, HD, -1).transpose(1, 0, 2, 3).reshape(H * HD, -1)
    wqkv = np.concatenate([q_order(a["L1_cond_Wq"]), a["L1_cond_Wk"], a["L1_cond_Wv"]], 0)
    wo = q_order(np.ascontiguousarray(a["L1_cond_Wo"].T))
    cache = np.stack([a["L1_cond_k_blocks"], a["L1_cond_v_blocks"]], 1)
    cache = cache.transpose(0, 3, 1, 2, 4).reshape(NPHYS * BLK, 2 * KW)
    arrays = {
        "x": a["x"].reshape(B * T, D),
        "kv_lens": a["itok_B_37_3939"].reshape(B, 1),
        "table": a["itok_Bx257_0_4111"],
        "cond": a["itok_B_1_198"].reshape(B, 1),
        "consts": consts,
        "cond_w": a["L0_cond_weights"],
        "gate_t": halves(a["L0_ffn_gate_weight"].T),
        "gate_a": a["L0_ffn_gate_lora_A"],
        "gate_bt": a["L0_ffn_gate_lora_B"].T,
        "gup": a["L0_ffn_gate_up_proj"].reshape(E0, 2, P, 2 * I0).transpose(2, 0, 1, 3).reshape(P, -1),
        "down": a["L0_ffn_down_proj"].transpose(1, 0, 2).reshape(I0, -1),
        "gup_a": a["L0_ffn_gup_lora_A"].transpose(1, 0, 2).reshape(R0, -1),
        "gup_bt": a["L0_ffn_gup_lora_B"].transpose(2, 0, 1).reshape(R0, -1),
        "down_a": a["L0_ffn_down_lora_A"].transpose(1, 0, 2).reshape(R0, -1),
        "down_bt": a["L0_ffn_down_lora_B"].transpose(2, 0, 1).reshape(R0, -1),
        "wqkv": halves(wqkv.T),
        "wo": halves(wo),
        "norm_scale": norm_rows(a["L1_cond_q_norm_scale"], a["L1_cond_k_norm_scale"]),
        "cache": cache,
        "router1": np.broadcast_to(a["L1_ffn_w_router"].reshape(1, -1), (P, E1 * D)),
        "fc": a["L1_ffn_w_fc"].transpose(0, 2, 1).reshape(E1, 2, P, H1).transpose(2, 0, 1, 3).reshape(P, -1),
        "proj": a["L1_ffn_w_proj"].transpose(0, 2, 1).reshape(E1, H1 // P, P, D).transpose(2, 0, 1, 3).reshape(P, -1),
    }
    arrays = {k: np.ascontiguousarray(v) for k, v in arrays.items()}
    nc = bacc.Bacc("TRN2", target_bir_lowering=False, num_devices=1)
    args = [nc.dram_tensor(f"in_{k}", v.shape, mybir.dt.from_np(v.dtype), kind="ExternalInput").ap()
            for k, v in arrays.items()]
    out = nc.dram_tensor("out_x", (B * T, D), F32, kind="ExternalOutput").ap()
    build(nc, at, *args, out)
    r = run(nc, [{f"in_{k}": v for k, v in arrays.items()}], core_ids=[0])
    return r.results[0]["out_x"].reshape(B, T, D)


def norm_rows(q_scale, k_scale):
    row = np.concatenate([np.tile(q_scale, H), np.tile(k_scale, G)])
    return np.broadcast_to(row[None, :], (P, QK))
```

```python
from contextlib import ExitStack

import numpy as np

import concourse.bass as bass
from concourse import mybir
from concourse.alu_op_type import AluOpType as ALU

F32 = mybir.dt.float32
I32 = mybir.dt.int32
ACT = mybir.ActivationFunctionType
AX = mybir.AxisListType

P = 128
B, T, D = 128, 32, 256
NT = B * T // P
BT = P // T
E0, I0, R0 = 8, 128, 16
E1, H1 = 2, 1024
N0 = (2 * B * T + E0 * (P - 1)) // P + 1
N1 = (B * T + E1 * (P - 1)) // P
H, G, HD = 8, 4, 32
KW = G * HD
BLK, NBLK, NPHYS = 16, 257, 4112
WIN = 128
NR = 11
NE = 3
KR = NR * BLK // 2
NK = 2 * KR
RING = 16
AHEAD = 12
KV_LAG = 10
NG = B // 8
NH = H + G
QK = NH * HD
SCALE = 256.0 ** -0.5
EPS = 1e-6
BIG = 65536.0
TWO_PI = 2 * np.pi
C1 = 6.28125
C2 = round((TWO_PI - C1) * 2 ** 20) / 2 ** 20
C3 = TWO_PI - C1 - C2


def constants():
    at, cols, n = {}, [], 0
    p = np.arange(P)

    def put(name, a):
        nonlocal n
        a = np.broadcast_to(np.asarray(a, np.float32), (P, np.shape(a)[-1]))
        at[name] = (n, n + a.shape[1])
        cols.append(a)
        n += a.shape[1]

    put("ident", np.eye(P))
    put("before", np.triu(np.ones((P, P)), 1))
    put("ones", np.ones((1, P)))
    put("rev8", 8.0 - np.arange(8))
    put("freq", (np.float32(1.0) / np.power(np.float32(10000.0), np.arange(16, dtype=np.float32) / np.float32(16))))
    key = (2 * np.arange(KR)[None, :] + np.arange(2)[:, None]).reshape(1, -1)
    put("keypos", key - (p % T)[:, None])
    put("entry", (NE * np.arange(B)[None, :] + np.arange(NE)[:, None] + 1).reshape(1, -1))
    put("slotno", np.arange(NBLK)[None, :])
    put("entry_of", NE * p[:, None] + np.arange(NE)[None, :] + 1)
    put("ahead", np.concatenate([np.arange(NE), np.arange(NR)])[None, :])
    put("row48", np.arange(NE * BLK)[None, :])
    put("off48", (np.arange(NE * BLK) % BLK)[None, :])
    put("pair", np.tile(np.arange(8), NR)[None, :])
    put("tokmod", (p % T)[:, None])
    put("tileno", np.arange(80)[None, :])
    put("eps", np.full((P, 1), EPS))
    return np.ascontiguousarray(np.concatenate(cols, 1)), at


class Chain:

    def __init__(self, eng, sem):
        self.eng, self.sem, self.base, self.n = eng, sem, 0, 0

    def mark(self, ins):
        self.n += 1
        ins.then_inc(self.sem, 1)

    def join(self):
        self.eng.wait_ge(self.sem, self.base + self.n)

    def link(self, ins):
        self.mark(ins)
        self.join()

    def enter(self, k, per_round):
        self.start = self.base + self.n
        self.base, self.n, self.per_round = self.start + k * per_round, 0, per_round

    def leave(self, rounds):
        assert self.n == self.per_round, (self.n, self.per_round)
        self.base, self.n = self.start + rounds * self.per_round, 0


class Step:

    def __init__(self, s, r, q, n, unroll, full):
        self.s, self.r, self.q, self.n, self.unroll, self.full = s, r, q, n, unroll, full

    def has(self, off):
        return self.full or 0 <= self.s + off < self.n

    def slot(self, off=0):
        return (self.q + off) % self.unroll

    def turn(self, off=0):
        return self.r + (self.q + off) // self.unroll


def skewed(eng, n, unroll, lead, lag, chain=None, per_round=0):
    rounds = (n - lead - lag) // unroll
    for s in range(-lead, lag):
        yield Step(s, s // unroll, s % unroll, n, unroll, False)
    with eng.Fori(0, rounds) as k:
        if chain:
            chain.enter(k, per_round)
        for u in range(lag, lag + unroll):
            yield Step(k * unroll + u, k + u // unroll, u % unroll, n, unroll, True)
        if chain:
            chain.leave(rounds)
    for s in range(lag + rounds * unroll, n + lag):
        yield Step(s, s // unroll, s % unroll, n, unroll, False)


def wait(eng, sem, value):
    if isinstance(value, int):
        if value <= 0:
            return
    else:
        assert value.min_val >= 1, value.min_val
    eng.wait_ge(sem, value)


def col(ap, i, n=1):
    return ap[:, bass.ds(i, n)]


def build(nc, at, x, kv_lens, table, cond, consts, cond_w, gate_t, gate_a, gate_bt, gup, down, gup_a, gup_bt,
          down_a, down_bt, wqkv, wo, norm_scale, cache, router1, fc, proj, out):
    with ExitStack() as ctx:
        def sb(name, shape, dt=F32):
            return ctx.enter_context(nc.sbuf_tensor(name, shape, dt))

        def dram(name, shape):
            return nc.dram_tensor(name, shape, F32, kind="Internal").ap()

        def sem(name):
            return ctx.enter_context(nc.semaphore(name))

        def sems(name, n):
            return [sem(f"{name}{i}") for i in range(n)]

        bank = [ctx.enter_context(nc.psum_tensor(f"bank{i}", [P, 512], F32)) for i in range(8)]

        cw_dram = dram("cond_w_by_batch", [B * T, T])
        slots0 = dram("slots0_in", [N0 * P, D])
        slots0_out = dram("slots0_out", [N0 * P, D])
        x1_dram = dram("x1_rows", [B * T, D])
        copies = dram("written_blocks", [NE * B * BLK, 2 * KW])
        slots1 = dram("slots1_in", [N1 * P, D])
        slots1_out = dram("slots1_out", [N1 * P, D])

        cst = sb("cst", [P, consts.shape[1]])
        rows = sb("rows", [P, NT * D])
        qt = sb("qt", [P, NT * 2 * P])
        experts = sb("experts", [P, 8192])
        kvring = sb("kvring", [P, RING * 4 * KW])
        work = sb("work", [P, 10240])
        wqkv_sb = sb("wqkv_sb", [P, 2 * 512])
        wo_sb = sb("wo_sb", [P, 2 * D])
        nscale = sb("nscale", [P, QK])
        wr1 = sb("wr1", [P, E1 * D])
        gate_sb = sb("gate_sb", [P, 2 * E0])
        gate_a_sb = sb("gate_a_sb", [R0, D])
        gate_bt_sb = sb("gate_bt_sb", [R0, E0])
        cosine = sb("cosine", [P, NT * 16])
        sine = sb("sine", [P, NT * 16])
        kv_i = sb("kv_i", [P, 1], I32)
        cond_i = sb("cond_i", [P, 1], I32)
        table_i = sb("table_i", [P, NBLK], I32)
        small_i = sb("small_i", [P, 16], I32)
        small = sb("small", [P, 96])
        index_work = sb("index_work", [P, 624])
        guard = sb("guard", [P, 1])
        entry_i = sb("entry_i", [P, NE], I32)
        dest_i = sb("dest_i", [P, NT], I32)
        read_i = sb("read_i", [KR, 2 * B], I32)
        delta = sb("delta", [P, B])
        logit0 = sb("logit0", [P, NT * E0])
        logit1 = sb("logit1", [P, NT * E1])
        route = sb("route", [P, 9 * 256])
        angle_i = route[:, 1024:1536].bitcast(I32)
        slot_i = sb("slot_i", [P, 3 * NT], I32)
        weight = sb("weight", [P, 3 * NT])
        tile_expert = sb("tile_expert", [P, 80])
        te0 = sb("te0", [P, 80], I32)
        te1 = sb("te1", [P, 80], I32)

        def c(name):
            a, b = at[name]
            return cst[:, a:b]

        ident = c("ident")

        s_const, s_int, s_lora, s_exp0, s_w, s_exp1 = (sem(n) for n in (
            "const_in", "ints_in", "lora_in", "experts0_in", "weights_in", "experts1_in"))
        s_cwg, s_cww, s_zero, s_zw, s_zw1 = (sem(n) for n in (
            "condw_gathered", "condw_written", "zeroed", "zeros0_written", "zeros1_written"))
        s_dv, s_ac = sem("dve_chain"), sem("act_chain")
        s_diag, s_er, s_cmp, s_cnt, s_turn, s_turned, s_idx = (sem(n) for n in (
            "diag_ready", "entry_rows_ready", "entry_compare_ready", "later_writers_counted", "turn_ready",
            "turned", "indices_ready"))
        s_blk, s_gate, s_gatec, s_ang, s_rope = (sem(n) for n in (
            "entry_blocks_ready", "gate_delta_ready", "gate_folded", "angles_ready", "rope_ready"))
        s_stg, s_stw = sem("block_staged"), sem("blocks_copied")
        s_fold, s_folded = sem("lora_product_ready"), sem("lora_folded")

        block = ctx.enter_context(nc.Block())

        xt = [work[:, k * 256:k * 256 + 256] for k in range(4)]
        bd = kvring[:, 0:NT * P]
        yt = [work[:, 1536 + k * 256:1792 + k * 256] for k in range(4)]
        scratch = work[:, 2560:10240]
        s1_in = sems("x_in", 4)
        s1_bd, s1_bd0, s1_yt, s1_y, s1_ytc, s1_yc, s1_lg, s1_lgc = (sem(n) for n in (
            "blockdiag_in", "blockdiag_zeroed", "y_turned_ready", "y_ready", "y_turned_copied", "y_copied", "logits_ready", "logits_copied"))
        s_oh, s_rank, s_slot, s_m, s_me = (sem(n) for n in (
            "onehot_ready", "ranks_ready", "slots_ready", "margin_ready", "margin_exp_ready"))
        s_sc0, s_sc1 = sem("rows_scattered0"), sem("rows_scattered1")
        xs = [work[:, k * 256:k * 256 + 256] for k in range(4)]
        xst = [work[:, 1024 + k * 256:1280 + k * 256] for k in range(2)]
        sg = [work[:, 1536 + k * 128:1664 + k * 128] for k in range(2)]
        ha = [work[:, 1792 + k * 128:1920 + k * 128] for k in range(2)]
        hat = [work[:, 2048 + k * 128:2176 + k * 128] for k in range(2)]
        os_ = [work[:, 2304 + k * 256:2560 + k * 256] for k in range(4)]
        s2_in, s2_out = sems("slot_tile_in", 4), sems("slot_tile_stored", 4)
        s2_t, s2_tc, s2_g, s2_sg, s2_a, s2_ta, s2_tac, s2_d, s2_dc = (sem("l0_" + n) for n in (
            "turned", "turned_copied", "gate_up", "silu", "hidden", "hidden_turned", "hidden_turned_copied",
            "down", "down_copied"))
        gbank = [bank[2], bank[3], bank[6], bank[7]]
        og = [[work[:, (2 * k + j) * 256:(2 * k + j) * 256 + 256] for j in range(2)] for k in range(4)]
        x1s = [work[:, 2048 + k * 256:2304 + k * 256] for k in range(4)]
        xr = [work[:, 3072 + k * 256:3328 + k * 256] for k in range(4)]
        qkv = [work[:, 4096 + k * 512:4608 + k * 512] for k in range(4)]
        x1t = [work[:, 6144 + k * 256:6400 + k * 256] for k in range(2)]
        sq = [work[:, 6656 + k * 384:7040 + k * 384] for k in range(2)]
        xn, xg, rc, rs = (work[:, 7424 + k * 384:7808 + k * 384] for k in range(4))
        x1a = work[:, 8960:9216]
        ms, sd, rinv = ([work[:, 9216 + k * 32 + j * 16:9228 + k * 32 + j * 16] for j in range(2)] for k in range(3))
        s3_og, s3_x, s3_st, s3_sc = sems("experts_out_in", 4), sems("x_again_in", 4), sems("x1_stored", 4), sems("kv_scattered", 4)
        s3_c, s3_t, s3_tc, s3_q, s3_sq, s3_v, s3_ms, s3_sd, s3_xn, s3_qk, s3_tq, s3_tqc = (sem("qkv_" + n) for n in (
            "combined", "turned", "turned_copied", "projected", "squared", "v_copied", "mean_square", "root",
            "normed", "roped", "q_turned", "q_turned_copied"))
        pbank = [bank[2], bank[3], bank[6], bank[7]]
        kv = [kvring[0:KR, k * 512:k * 512 + 512] for k in range(RING)]
        qbd = [work[:, k * 1024:k * 1024 + 1024] for k in range(2)]
        kt = [work[:, 2048 + k * 176:2224 + k * 176] for k in range(2)]
        dist = [work[:, 2400 + k * 176:2576 + k * 176] for k in range(2)]
        pen = [work[:, 2752 + k * 176:2928 + k * 176] for k in range(2)]
        sc = [work[:, 3104 + k * 352:3456 + k * 352] for k in range(2)]
        pr = [work[:, 3808 + k * 352:4160 + k * 352] for k in range(2)]
        pn = [work[:, 4512 + k * 352:4864 + k * 352] for k in range(2)]
        pt = [work[0:KR, 5216 + k * 512:5728 + k * 512] for k in range(2)]
        ot = [work[:, 6240 + k * 256:6496 + k * 256] for k in range(2)]
        mx, ng, sm, ri = ([work[:, 6752 + k * 8 + j * 4:6754 + k * 8 + j * 4] for j in range(2)] for k in range(4))
        junk = [work[:, 6784 + k * 256:7040 + k * 256] for k in range(2)]
        s4_in = sems("cache_rows_in", RING)
        (s4_z, s4_qbd, s4_kt, s4_ktc, s4_s, s4_di, s4_pen, s4_ttr, s4_ng, s4_ex, s4_ri, s4_pn, s4_tp, s4_tpc, s4_pv,
         s4_oc, s4_w, s4_wc) = (sem("att_" + n) for n in (
             "q_zeroed", "q_spread", "k_turned", "k_turned_copied", "scores", "distance", "penalty", "masked",
             "negmax", "exp", "recip", "probs", "probs_turned", "probs_turned_copied", "pv", "o_copied", "projected",
             "projected_copied"))
        ys = [work[:, k * 256:k * 256 + 256] for k in range(4)]
        yst = [work[:, 1024 + k * 256:1280 + k * 256] for k in range(2)]
        half = [work[:, 1536 + k * 512:2048 + k * 512] for k in range(2)]
        lk = [work[:, 2560 + k * 512:3072 + k * 512] for k in range(2)]
        av = [work[:, 3584 + k * 512:4096 + k * 512] for k in range(2)]
        avt = [work[:, 4608 + k * 512:5120 + k * 512] for k in range(2)]
        zs = [work[:, 5632 + k * 256:5888 + k * 256] for k in range(4)]
        s6_in, s6_out = sems("slot1_tile_in", 4), sems("slot1_tile_stored", 2)
        s6_t, s6_tc, s6_f, s6_h, s6_l, s6_a, s6_ta, s6_tac, s6_p, s6_pc = (sem("l1_" + n) for n in (
            "turned", "turned_copied", "fc", "halved", "leaky", "squared", "hidden_turned", "hidden_turned_copied",
            "proj", "proj_copied"))
        zg = [work[:, k * 256:k * 256 + 256] for k in range(4)]
        x1r = [work[:, 1024 + k * 256:1280 + k * 256] for k in range(4)]
        res = [work[:, 2048 + k * 256:2304 + k * 256] for k in range(4)]
        s7_g, s7_x, s7_st, s7_r = sems("expert1_out_in", 4), sems("x1_in", 4), sems("result_stored", 4), sem("result_ready")

        gup_v = experts[:, 0:E0 * 512]
        down_v = experts[:, E0 * 512:E0 * 768]
        fc_v = experts[:, 0:E1 * 2048]
        proj_v = experts[:, E1 * 2048:E1 * 4096]
        lora_gup_a, lora_gup_b = qt[0:R0, 0:2048], qt[0:R0, 2048:4096]
        lora_down_a, lora_down_b = qt[0:R0, 4096:5120], qt[0:R0, 5120:7168]
        copies_blocks = copies.rearrange("(b k r) f -> k b (r f)", k=NE, r=BLK)
        copies_pairs = copies.rearrange("(n r) f -> n (r f)", r=2)
        cache_blocks = cache.rearrange("(n r) f -> n (r f)", r=BLK)
        cache_pairs = cache.rearrange("(n r) f -> n (r f)", r=2)
        block_buffer = kvring[:, 4096:8192]
        cw_buffer = rows[:, 0:T * T]

        diag = scratch[:, 5376:5888]
        later = scratch[:, 6272:6272 + NE * NE * B]
        covers = index_work[:, 256:304]
        dest_b, read_b = index_work[:, 320:448], index_work[:, 448:624]
        onehot0, onehot1 = route[:, 1024:1280], route[:, 1024:1024 + 2 * E1]

        def stage3_drained(eng):
            eng.wait_ge(s3_tq, NT)
            for k in range(4):
                eng.wait_ge(s3_st[k], 16 * NT // 4)
                eng.wait_ge(s3_sc[k], 16 * NT // 4)

        @block.sync
        def _(sp):
            sp.dma_start(cst[:], consts).then_inc(s_const, 16)
            sp.dma_start(cond_i[:], cond).then_inc(s_int, 16)
            sp.dma_start(kv_i[:], kv_lens).then_inc(s_int, 16)
            sp.dma_start(table_i[:], table).then_inc(s_int, 16)
            sp.dma_start(gate_sb[:], gate_t).then_inc(s_w, 16)
            sp.dma_start(gate_a_sb[:], gate_a).then_inc(s_w, 16)
            sp.dma_start(gate_bt_sb[:], gate_bt).then_inc(s_w, 16)
            sp.wait_ge(s_cwg, 16)
            sp.dma_start(cw_dram.rearrange("(b c) d -> b (c d)", b=B), cw_buffer).then_inc(s_cww, 16)
            sp.wait_ge(s_cww, 16)
            sp.wait_ge(s1_bd0, 1)
            for j in range(BT):
                sp.dma_start(bd[T * j:T * j + T, :].rearrange("c (i d) -> c i d", i=NT)[:, :, T * j:T * j + T],
                             cw_dram.rearrange("(i j c) d -> j c i d", j=BT, c=T)[j]).then_inc(s1_bd, 16)
            for st in skewed(sp, NT, 4, 0, 4):
                if not st.has(0):
                    continue
                wait(sp, s1_yt, st.s - 3)
                sp.dma_start(xt[st.q], x[bass.ds(st.s * P, P), :]).then_inc(s1_in[st.q], 16)
            sp.wait_ge(s_sc0, 16 * 2 * NT)
            for st in skewed(sp, N0, 4, 3, 9):
                if st.has(3):
                    wait(sp, s2_t, st.s)
                    sp.dma_start(xs[st.slot(3)], slots0[bass.ds((st.s + 3) * P, P), :]).then_inc(s2_in[st.slot(3)], 16)
                if st.has(-8):
                    sp.wait_ge(s2_dc, st.s - 7)
                    sp.dma_start(slots0_out[bass.ds((st.s - 8) * P, P), :], os_[st.slot(-8)]).then_inc(
                        s2_out[st.slot(-8)], 16)
            sp.wait_ge(s2_d, N0)
            sp.dma_start(fc_v, fc).then_inc(s_exp1, 16)
            sp.dma_start(proj_v, proj).then_inc(s_exp1, 16)
            for k in range(4):
                sp.wait_ge(s2_out[k], 16 * ((N0 + 3 - k) // 4))
            for st in skewed(sp, NT, 4, 3, 5):
                if st.has(3):
                    wait(sp, s3_c, st.s)
                    sp.dma_start(xr[st.slot(3)], x[bass.ds((st.s + 3) * P, P), :]).then_inc(s3_x[st.slot(3)], 16)
                if st.has(-1):
                    sp.wait_ge(s3_c, st.s)
                    sp.dma_start(x1_dram[bass.ds((st.s - 1) * P, P), :], x1s[st.slot(-1)]).then_inc(
                        s3_st[st.slot(-1)], 16)
            sp.wait_ge(s_sc1, 16 * NT)
            for st in skewed(sp, N1, 4, 3, 4):
                if st.has(3):
                    wait(sp, s6_t, st.s)
                    sp.dma_start(ys[st.slot(3)], slots1[bass.ds((st.s + 3) * P, P), :]).then_inc(s6_in[st.slot(3)], 16)
                if st.has(-3):
                    q = st.slot(-3) % 2
                    sp.wait_ge(s6_pc, st.s - 2)
                    sp.dma_start(slots1_out[bass.ds((st.s - 3) * P, P), :], zs[q]).then_inc(s6_out[q], 16)
            for k in range(4):
                sp.wait_ge(s3_st[k], 16 * NT // 4)
            for k in range(2):
                sp.wait_ge(s6_out[k], 16 * ((N1 + 1 - k) // 2))
            for st in skewed(sp, NT, 4, 3, 5):
                if st.has(3):
                    wait(sp, s7_r, st.s)
                    sp.dma_start(x1r[st.slot(3)], x1_dram[bass.ds((st.s + 3) * P, P), :]).then_inc(s7_x[st.slot(3)], 16)
                if st.has(-1):
                    sp.wait_ge(s7_r, st.s)
                    sp.dma_start(out[bass.ds((st.s - 1) * P, P), :], res[st.slot(-1)]).then_inc(s7_st[st.slot(-1)], 16)
            for k in range(4):
                sp.wait_ge(s7_st[k], 16 * NT // 4)

        @block.gpsimd
        def _(pool):
            def gather(dst, src, index, done, bound=None):
                kw = {} if bound is None else {"bounds_check": bound, "oob_is_err": False}
                pool.indirect_dma_start(dst, None, src, bass.IndirectOffsetOnAxis(ap=index, axis=0), **kw).then_inc(done, 16)

            def scatter(dst, src, index, done, bound=None):
                kw = {} if bound is None else {"bounds_check": bound, "oob_is_err": False}
                pool.indirect_dma_start(dst, bass.IndirectOffsetOnAxis(ap=index, axis=0), src, None, **kw).then_inc(done, 16)

            pool.wait_ge(s_int, 48)
            gather(cw_buffer, cond_w.rearrange("s c d -> s (c d)"), cond_i[:, 0:1], s_cwg)
            pool.wait_ge(s_slot, 1)
            pool.wait_ge(s1_yc, NT)
            pool.wait_ge(s_zw, 16 * (NT // 4))
            for i in range(NT):
                for j in range(2):
                    scatter(slots0, rows[:, i * D:i * D + D], slot_i[:, j * NT + i:j * NT + i + 1], s_sc0)
            pool.wait_ge(s_blk, 1)
            for k in range(NE):
                if k:
                    pool.wait_ge(s_stw, 16 * k)
                gather(block_buffer, cache_blocks, entry_i[:, k:k + 1], s_stg)
                pool.wait_ge(s_stg, 16 * (k + 1))
                pool.dma_start(copies_blocks[k], block_buffer).then_inc(s_stw, 16)
            pool.wait_ge(s_stw, 16 * NE)
            pool.wait_ge(s_idx, 1)
            for b in range(RING):
                gather(kv[b], cache_pairs, read_i[:, b:b + 1], s4_in[b], NPHYS * 8 - 1)
            for k in range(4):
                pool.wait_ge(s2_out[k], 16 * ((N0 + 3 - k) // 4))
            for i in range(NT + KV_LAG):
                if i < NT:
                    wait(pool, s3_c, i - 3)
                    for j in range(2):
                        gather(og[i % 4][j], slots0_out, slot_i[:, j * NT + i:j * NT + i + 1], s3_og[i % 4])
                t = i - KV_LAG
                if t >= 0:
                    pool.wait_ge(s3_qk, t + 1)
                    pool.wait_ge(s3_v, t + 1)
                    scatter(copies, qkv[t % 4][:, 2 * P:512], dest_i[:, t:t + 1], s3_sc[t % 4],
                            NE * B * BLK - 1)
            for k in range(4):
                pool.wait_ge(s3_sc[k], 16 * NT // 4)
            pool.wait_ge(s_zw1, 16)

            def scatter_tile(i):
                pool.wait_ge(s_slot, i // 2 + 2)
                pool.wait_ge(s4_wc, i + 1)
                scatter(slots1, rows[:, i * D:i * D + D], slot_i[:, 2 * NT + i:2 * NT + i + 1], s_sc1)

            SCATTER_LAG = 32
            for b in range(RING - AHEAD, B + RING - AHEAD):
                if RING <= b < B:
                    pool.wait_ge(s4_pv, b - RING + 1)
                    gather(kv[b % RING], cache_pairs, read_i[:, b:b + 1], s4_in[b % RING], NPHYS * 8 - 1)
                c0 = b - (RING - AHEAD)
                pool.wait_ge(s4_in[c0 % RING], 32 * (c0 // RING) + 16)
                gather(kv[c0 % RING], copies_pairs, read_i[:, B + c0:B + c0 + 1], s4_in[c0 % RING], NE * B * 8 - 1)
                if b >= SCATTER_LAG and (b - SCATTER_LAG) % 4 == 0:
                    scatter_tile((b - SCATTER_LAG) // 4)
            for i in range((B + RING - AHEAD - 1 - SCATTER_LAG) // 4 + 1, NT):
                scatter_tile(i)
            for k in range(2):
                pool.wait_ge(s6_out[k], 16 * ((N1 + 1 - k) // 2))
            for i in range(NT):
                wait(pool, s7_r, i - 3)
                gather(zg[i % 4], slots1_out, slot_i[:, 2 * NT + i:2 * NT + i + 1], s7_g[i % 4])

        @block.scalar
        def _(act):
            ch = Chain(act, s_ac)
            act.dma_start(wqkv_sb[:], wqkv).then_inc(s_w, 16)
            act.dma_start(wo_sb[:], wo).then_inc(s_w, 16)
            act.dma_start(nscale[:], norm_scale).then_inc(s_w, 16)
            act.dma_start(wr1[:], router1).then_inc(s_w, 16)
            act.dma_start(lora_gup_a, gup_a).then_inc(s_lora, 16)
            act.dma_start(lora_gup_b, gup_bt).then_inc(s_lora, 16)
            act.dma_start(lora_down_a, down_a).then_inc(s_lora, 16)
            act.dma_start(lora_down_b, down_bt).then_inc(s_lora, 16)
            act.wait_ge(s_cww, 16)
            act.wait_ge(s1_in[3], 16)
            act.dma_start(gup_v, gup).then_inc(s_exp0, 16)
            act.dma_start(down_v, down).then_inc(s_exp0, 16)
            act.wait_ge(s_zero, 1)
            zeros = scratch[:, 7424:7680]
            slot_tiles = lambda dst: dst.rearrange("(n p) d -> p n d", p=P)
            NZ = N0 * 4 // NT
            for st in skewed(act, NT, 4, 0, 0):
                if st.q == 0:
                    act.dma_start(slot_tiles(slots0)[:, bass.ds(st.turn() * NZ, NZ), :],
                                  zeros[:, None, :].broadcast_to([P, NZ, D])).then_inc(s_zw, 16)
                act.wait_ge(s1_y, st.s + 1)
                act.activation(col(rows, st.s * D, D), bank[2 + st.q % 2][:, 0:D], ACT.Copy).then_inc(s1_yc, 1)
            act.wait_ge(s_m, 1)
            act.activation(weight[:, NT:2 * NT], weight[:, NT:2 * NT], ACT.Exp).then_inc(s_me, 1)
            act.dma_start(slot_tiles(slots1), zeros[:, None, :].broadcast_to([P, N1, D])).then_inc(s_zw1, 16)
            act.wait_ge(s_ang, 1)
            act.activation(sine[:], sine[:], ACT.Sin).then_inc(s_rope, 1)
            act.activation(cosine[:], cosine[:], ACT.Sin).then_inc(s_rope, 1)
            for st in skewed(act, N0, 4, 3, 5):
                if st.has(0):
                    q = st.q % 2
                    act.wait_ge(s2_g, st.s + 1)
                    wait(act, s2_a, st.s - 1)
                    act.activation(sg[q], gbank[st.q][:, 0:I0], ACT.Silu).then_inc(s2_sg, 1)
                if st.has(-3):
                    q = st.slot(-3) % 2
                    act.wait_ge(s2_ta, st.s - 2)
                    wait(act, s2_d, st.s - 4)
                    act.activation(hat[q], bank[4 + q][:, 0:P], ACT.Copy).then_inc(s2_tac, 1)
            for st in skewed(act, NT, 4, 2, 6):
                if st.has(1):
                    q = st.slot(1) % 2
                    act.wait_ge(s3_t, st.s + 2)
                    wait(act, s3_q, st.s)
                    act.activation(x1t[q], bank[q][:, 0:D], ACT.Copy).then_inc(s3_tc, 1)
                if st.has(-1):
                    q = st.slot(-1)
                    act.wait_ge(s3_q, st.s)
                    wait(act, s3_ms, st.s - 2)
                    act.activation(sq[q % 2], pbank[q][:, 0:QK], ACT.Square).then_inc(s3_sq, 1)
                if st.has(-5):
                    act.wait_ge(s3_tq, st.s - 4)
                    act.activation(col(qt, (st.s - 5) * 2 * P, 2 * P), bank[4 + st.slot(-5) % 2][:, 0:2 * P],
                                   ACT.Copy).then_inc(s3_tqc, 1)
                if st.has(-2):
                    q = st.slot(-2)
                    act.wait_ge(s3_q, st.s - 1)
                    wait(act, s3_sc[q], 16 * st.turn(-2))
                    act.activation(qkv[q][:, QK:512], pbank[q][:, QK:512], ACT.Copy).then_inc(s3_v, 1)
                    act.wait_ge(s3_ms, st.s - 1)
                    wait(act, s3_xn, st.s - 3)
                    act.activation(sd[q % 2], ms[q % 2], ACT.Sqrt, bias=c("eps"), scale=1.0 / HD).then_inc(s3_sd, 1)
            stage3_drained(act)
            act.wait_ge(s_idx, 1)
            act.wait_ge(s4_z, 1)
            act.wait_ge(s3_tqc, NT)
            for st in skewed(act, B, 8, 4, 9):
                if st.has(-1):
                    q = st.slot(-1) % 2
                    act.wait_ge(s4_ng, st.s)
                    wait(act, s4_pn, st.s - 2)
                    for g in range(2):
                        act.activation(pr[q][:, g * NK:g * NK + NK], sc[q][:, g * NK:g * NK + NK], ACT.Exp,
                                       bias=ng[q][:, g:g + 1], scale=SCALE, accum_out=sm[q][:, g:g + 1]).then_inc(s4_ex, 1)
                if st.has(2):
                    q = st.slot(2) % 2
                    act.wait_ge(s4_kt, st.s + 3)
                    wait(act, s4_s, st.s + 1)
                    act.activation(kt[q], bank[q][:, 0:NK], ACT.Copy).then_inc(s4_ktc, 1)
                    wait(act, s4_pen, st.s + 1)
                    act.activation(dist[q], c("keypos"), ACT.Abs, bias=col(delta, st.s + 2)).then_inc(s4_di, 1)
                if st.q % 4 == 0 and st.has(4):
                    tile, t = 2 * st.turn(4) + st.slot(4) // 4, st.slot(4) // 4
                    wait(act, s4_s, st.s)
                    for g in range(G):
                        p0 = HD * g
                        src = qt[p0:p0 + HD, bass.ds(tile * 2 * P, 2 * P)].rearrange("p (h b t) -> p b h t", h=2, b=BT)
                        dst = qbd[t][p0:p0 + HD, :].rearrange("p (b g h t) -> p b g h t", b=BT, g=G, h=2)[:, :, g, :, :]
                        act.activation(dst, src, ACT.Copy).then_inc(s4_qbd, 1)
                if st.q % 2 == 1 and st.has(-6):
                    pair = st.slot(-7) // 2 % 2
                    act.wait_ge(s4_pv, st.s - 5)
                    dst = ot[st.slot(-7) // 4].rearrange("p (h b t) -> p b h t", h=2, b=BT)
                    src = bank[6 + pair][:, :].rearrange("p (b g h t) -> p b g h t", b=2, g=G, h=2)
                    for g in range(G):
                        act.activation(dst[HD * g:HD * g + HD, 2 * pair:2 * pair + 2, :, :],
                                       src[HD * g:HD * g + HD, :, g, :, :], ACT.Copy).then_inc(s4_oc, 1)
                if st.q % 4 == 3 and st.has(-8):
                    tile = 2 * st.turn(-8) + st.slot(-8) // 4
                    act.wait_ge(s4_w, tile + 1)
                    act.activation(col(rows, tile * D, D), bank[1][:, D:2 * D], ACT.Copy).then_inc(s4_wc, 1)
            act.wait_ge(s_m, 2)
            act.activation(weight[:, 2 * NT:3 * NT], weight[:, 2 * NT:3 * NT], ACT.Exp).then_inc(s_me, 1)
            for st in skewed(act, 2 * N1, 4, 3, 2):
                if st.q % 2 == 1 and st.has(3):
                    tile, t = 2 * st.turn(3) + st.slot(3) // 2, st.slot(3) // 2
                    act.wait_ge(s6_t, tile + 1)
                    wait(act, s6_f, 2 * tile - 2)
                    act.activation(yst[t], bank[7 * t][:, 0:D], ACT.Copy).then_inc(s6_tc, 1)
                if st.has(2):
                    h = st.s + 2
                    act.wait_ge(s6_f, h + 1)
                    wait(act, s6_l, h - 1)
                    act.activation(half[st.slot(2) % 2], bank[1 + st.slot(2) % 2][:, :], ACT.Copy, scale=0.5).then_inc(s6_h, 1)
                    act.wait_ge(s6_l, h + 1)
                    wait(act, s6_ta, h - 1)
                    act.activation(av[st.slot(2) % 2], lk[st.slot(2) % 2], ACT.Square).then_inc(s6_a, 1)

        @block.tensor
        def _(pe):
            pe.wait_ge(s_const, 16)
            pe.wait_ge(s_w, 16 * 7)
            for h in range(2):
                mm = pe.matmul(bank[3][:, h * E0:h * E0 + E0], gate_a_sb[:, h * P:h * P + P], gate_bt_sb[:, :],
                               start=True, stop=True)
            mm.then_inc(s_gate, 1)
            pe.wait_ge(s1_bd, 16 * BT)
            pe.wait_ge(s_gatec, 1)
            for st in skewed(pe, NT, 4, 2, 4):
                if st.has(2):
                    q = st.slot(2)
                    pe.wait_ge(s1_in[q], 16 * st.turn(2) + 16)
                    wait(pe, s1_ytc, st.s + 1)
                    for h in range(2):
                        mm = pe.matmul(bank[q % 2][:, h * P:h * P + P], xt[q][:, h * P:h * P + P],
                                       bd[:, bass.ds((st.s + 2) * P, P)], start=True, stop=True)
                    mm.then_inc(s1_yt, 1)
                if st.has(0):
                    pe.wait_ge(s1_ytc, st.s + 1)
                    wait(pe, s1_yc, st.s - 1)
                    for h in range(2):
                        mm = pe.transpose(bank[2 + st.q % 2][:, h * P:h * P + P], yt[st.q][:, h * P:h * P + P], ident)
                    mm.then_inc(s1_y, 1)
                    wait(pe, s1_lgc, st.s - 1)
                    for h in range(2):
                        mm = pe.matmul(bank[4 + st.q % 2][:, 0:E0], yt[st.q][:, h * P:h * P + P],
                                       gate_sb[:, h * E0:h * E0 + E0], start=(h == 0), stop=(h == 1))
                    mm.then_inc(s1_lg, 1)

            def ranks(onehot, n, turn):
                pe.wait_ge(s_oh, turn)
                pe.matmul(bank[6][:, 0:n], c("before"), onehot, start=True, stop=True)
                pe.matmul(bank[7][:, 0:n], c("ones"), onehot, start=True, stop=True).then_inc(s_rank, 1)

            ranks(onehot0, NT * E0, 1)
            pe.wait_ge(s_lora, 64)
            pe.wait_ge(s1_yc, NT)
            for e in range(E0):
                wait(pe, s_folded, 2 * (e - 1))
                for h in range(2):
                    pe.matmul(bank[e % 2][:, h * 256:h * 256 + 256], lora_gup_a[:, e * D + h * P:e * D + h * P + P],
                              lora_gup_b[:, e * 256:e * 256 + 256], start=True, stop=True)
                pe.matmul(bank[2 + e % 2][:, 0:D], lora_down_a[:, e * I0:e * I0 + I0],
                          lora_down_b[:, e * D:e * D + D], start=True, stop=True).then_inc(s_fold, 1)
            pe.wait_ge(s_folded, 2 * E0)
            pe.wait_ge(s_diag, 1)
            pe.matmul(bank[0][:, :], c("ones"), diag, start=True, stop=True).then_inc(s_er, 1)
            pe.wait_ge(s_cmp, 1)
            for k in range(NE):
                for k2 in range(NE):
                    mm = pe.matmul(bank[1][:, BLK * k:BLK * k + BLK], later[:, k2 * NE * B + k * B:k2 * NE * B + k * B + B],
                                   covers[:, BLK * k2:BLK * k2 + BLK], start=(k2 == 0), stop=(k2 == NE - 1))
            mm.then_inc(s_cnt, 1)
            pe.wait_ge(s_turn, 1)
            pe.transpose(bank[2][:, 0:P], dest_b, ident)
            for w in range(2):
                pe.transpose(bank[2][0:KR, P + w * B:P + w * B + B], read_b[:, w * KR:w * KR + KR], ident)
            pe.matmul(bank[2][:, 3 * P:4 * P], c("ones"), diag[:, 0:P], start=True, stop=True).then_inc(s_turned, 1)
            pe.wait_ge(s_idx, 1)
            def expert_of(te, tile, n):
                v = pe.value_load(te[0:1, bass.ds(tile, 1)])
                return nc.s_assert_within(v, 0, n - 1, skip_runtime_bounds_check_because="tile experts are clamped")

            for st in skewed(pe, N0, 4, 3, 6):
                if st.has(-4):
                    q = st.slot(-4) % 2
                    expert = expert_of(te0, st.s - 4, E0)
                    weights = down_v[:, bass.ds(expert * 256, 256)]
                    pe.wait_ge(s2_tac, st.s - 3)
                    pe.wait_ge(s2_tc, st.s + 2 if st.full else min(st.s + 2, N0))
                    wait(pe, s2_dc, st.s - 5)
                    pe.matmul(bank[st.q % 2][:, D:2 * D], hat[q], weights, start=True, stop=True).then_inc(s2_d, 1)
                if st.has(1):
                    q = st.slot(1)
                    expert = expert_of(te0, st.s + 1, E0)
                    weights = [gup_v[:, h * 256:][:, bass.ds(expert * 512, 256)] for h in range(2)]
                    pe.wait_ge(s2_tc, st.s + 2)
                    wait(pe, s2_a, st.s - 2)
                    for h in range(2):
                        mm = pe.matmul(gbank[q][:, 0:256], xst[q % 2][:, h * P:h * P + P], weights[h],
                                       start=(h == 0), stop=(h == 1))
                    mm.then_inc(s2_g, 1)
                if st.has(3):
                    q = st.slot(3)
                    pe.wait_ge(s2_in[q], 16 * st.turn(3) + 16)
                    wait(pe, s2_tc, st.s + 2)
                    for h in range(2):
                        mm = pe.transpose(bank[st.q % 2][:, h * P:h * P + P], xs[q][:, h * P:h * P + P], ident)
                    mm.then_inc(s2_t, 1)
                if st.has(-2):
                    q = st.q % 2
                    pe.wait_ge(s2_a, st.s - 1)
                    wait(pe, s2_tac, st.s - 3)
                    pe.transpose(bank[4 + q][:, 0:P], ha[q], ident).then_inc(s2_ta, 1)
            for st in skewed(pe, NT, 4, 2, 6):
                if st.has(0):
                    q = st.q % 2
                    pe.wait_ge(s3_tc, st.s + 1)
                    wait(pe, s3_xn, st.s - 3)
                    for h in range(2):
                        mm = pe.matmul(pbank[st.q][:, :], x1t[q][:, h * P:h * P + P], wqkv_sb[:, h * 512:h * 512 + 512],
                                       start=(h == 0), stop=(h == 1))
                    mm.then_inc(s3_q, 1)
                if st.has(-4):
                    q = st.slot(-4)
                    pe.wait_ge(s3_qk, st.s - 3)
                    wait(pe, s3_tqc, st.s - 5)
                    for h in range(2):
                        mm = pe.transpose(bank[4 + q % 2][:, h * P:h * P + P], qkv[q][:, h * P:h * P + P], ident)
                    mm.then_inc(s3_tq, 1)
                if st.has(2):
                    q = st.slot(2)
                    pe.wait_ge(s3_c, st.s + 3)
                    wait(pe, s3_tc, st.s + 1)
                    for h in range(2):
                        mm = pe.transpose(bank[q % 2][:, h * P:h * P + P], x1s[q][:, h * P:h * P + P], ident)
                    mm.then_inc(s3_t, 1)
            for st in skewed(pe, B, RING, 4, 13):
                if st.has(-5):
                    q = st.slot(-5)
                    pe.wait_ge(s4_tpc, st.s - 4)
                    if q % 2 == 0:
                        wait(pe, s4_oc, 2 * (st.s - 7))
                    for r in range(2):
                        mm = pe.matmul(bank[6 + q // 2 % 2][:, (q % 2) * 256:(q % 2) * 256 + 256],
                                       kv[q][:, r * 256 + KW:r * 256 + 2 * KW], pt[q % 2][:, r * 256:r * 256 + 256],
                                       start=(r == 0), stop=(r == 1))
                    mm.then_inc(s4_pv, 1)
                if st.has(-3):
                    q = st.slot(-3)
                    pe.wait_ge(s4_pn, st.s - 2)
                    wait(pe, s4_tpc, st.s - 4)
                    for r in range(2):
                        for g in range(2):
                            mm = pe.transpose(bank[4 + q % 2][0:KR, (2 * r + g) * P:(2 * r + g) * P + P],
                                              pn[q % 2][:, g * NK + r * KR:g * NK + r * KR + KR], ident)
                    mm.then_inc(s4_tp, 1)
                if st.q % 8 == 1 and st.has(-10):
                    g = 2 * st.turn(-10) + st.slot(-10) // 8
                    pe.wait_ge(s_oh, g + 2)
                    pe.wait_ge(s4_ng, st.s if st.full else min(st.s, B))
                    pe.matmul(bank[2][:, 384:384 + 2 * E1], c("before"), onehot1, start=True, stop=False)
                    pe.matmul(bank[2][:, 384 + E1:384 + 2 * E1], c("ones"), onehot1[:, 0:E1], start=False, stop=True)
                    for i in range(2):
                        mm = pe.matmul(bank[2][:, 400:400 + E1], c("ones"), onehot1[:, i * E1:i * E1 + E1],
                                       start=(i == 0), stop=(i == 1))
                    mm.then_inc(s_rank, 1)
                if st.has(1):
                    q, tile = st.slot(1), 4 * st.turn(1) + st.slot(1) // 4
                    if st.q % 8 == 3 and st.has(-12):
                        pe.wait_ge(s_slot, 2 * st.turn(-12) + st.slot(-12) // 8 + 2)
                    pe.wait_ge(s4_ktc, st.s + 2)
                    pe.wait_ge(s4_qbd, G * (tile + 1))
                    wait(pe, s4_ng, st.s)
                    for g in range(2):
                        mm = pe.matmul(bank[2 + q % 2][:, g * NK:g * NK + NK],
                                       qbd[q // 4 % 2][:, (q % 4) * 256 + g * P:(q % 4) * 256 + g * P + P], kt[q % 2],
                                       start=True, stop=True)
                    mm.then_inc(s4_s, 1)
                if st.q % 4 == 2 and st.has(-7):
                    tile, t = 4 * st.turn(-7) + st.slot(-7) // 4, st.slot(-7) // 4 % 2
                    pe.wait_ge(s4_oc, 2 * G * (tile + 1))
                    if not st.full:
                        wait(pe, s4_ktc, min(st.s + 2, B))
                    wait(pe, s4_wc, tile)
                    for h in range(2):
                        mm = pe.matmul(bank[1][:, D:2 * D], ot[t][:, h * P:h * P + P], wo_sb[:, h * D:h * D + D],
                                       start=(h == 0), stop=(h == 1))
                    mm.then_inc(s4_w, 1)
                if st.has(3):
                    q = st.slot(3)
                    pe.wait_ge(s4_in[q], 32 * st.turn(3) + 32)
                    if not st.full and st.s < -1:
                        pe.wait_ge(s3_tqc, NT)
                    wait(pe, s4_ktc, st.s + 2)
                    if st.q % 4 == 0 and st.has(-9):
                        pe.wait_ge(s4_wc, 4 * st.turn(-9) + st.slot(-9) // 4 + 1)
                    for r in range(2):
                        mm = pe.transpose(bank[q % 2][:, r * KR:r * KR + KR], kv[q][:, r * 256:r * 256 + KW], ident[0:KR, 0:KR])
                    mm.then_inc(s4_kt, 1)
            pe.wait_ge(s_exp1, 32)
            pe.wait_ge(s_slot, NG + 2)
            for st in skewed(pe, 2 * N1, 8, 4, 4):
                if st.has(2):
                    n, t, tile = st.slot(2) % 2, st.slot(2) // 2 % 2, 4 * st.turn(2) + st.slot(2) // 2
                    if n == 0:
                        fc_expert = expert_of(te1, tile, E1) * 2048
                    weights = [fc_v[:, h * H1 + n * 512:][:, bass.ds(fc_expert, 512)] for h in range(2)]
                    pe.wait_ge(s6_tc, tile + 1)
                    wait(pe, s6_l, st.s + 1)
                    for h in range(2):
                        mm = pe.matmul(bank[1 + n][:, :], yst[t][:, h * P:h * P + P],
                                       weights[h], start=(h == 0), stop=(h == 1))
                    mm.then_inc(s6_f, 1)
                if st.has(0):
                    n, t, tile = st.q % 2, st.q // 2 % 2, 4 * st.turn() + st.q // 2
                    if n == 0:
                        proj_expert = expert_of(te1, tile, E1) * 2048
                    weights = [proj_v[:, (4 * n + k) * D:][:, bass.ds(proj_expert, D)] for k in range(4)]
                    pe.wait_ge(s6_tac, st.s + 1)
                    if n == 0:
                        wait(pe, s6_pc, tile - 1)
                    for k in range(4):
                        mm = pe.matmul(bank[5 + t][:, 0:D], avt[n][:, k * P:k * P + P],
                                       weights[k],
                                       start=(n == 0 and k == 0), stop=(n == 1 and k == 3))
                    mm.then_inc(s6_p, 1)
                if st.has(1):
                    n = st.slot(1) % 2
                    pe.wait_ge(s6_a, st.s + 2)
                    wait(pe, s6_tac, st.s)
                    for k in range(4):
                        mm = pe.transpose(bank[3 + n][:, k * P:k * P + P], av[n][:, k * P:k * P + P], ident)
                    mm.then_inc(s6_ta, 1)
                if st.q % 2 == 0 and st.has(4):
                    t, tile = st.slot(4) // 2, 4 * st.turn(4) + st.slot(4) // 2
                    pe.wait_ge(s6_in[t], 16 * st.turn(4) + 16)
                    wait(pe, s6_tc, tile - 1)
                    for h in range(2):
                        mm = pe.transpose(bank[7 * (t % 2)][:, h * P:h * P + P], ys[t][:, h * P:h * P + P], ident)
                    mm.then_inc(s6_t, 1)

        @block.vector
        def _(dve):
            ch = Chain(dve, s_dv)
            link = ch.link
            dve.memset(bd, 0.0).then_inc(s1_bd0, 1)
            dve.memset(scratch[:, 7424:7680], 0.0).then_inc(s_zero, 1)
            dve.wait_ge(s_const, 16)
            dve.wait_ge(s_int, 48)

            length, first, last_off = small[:, 0:1], small[:, 2:3], small[:, 4:5]
            start = small[:, 5:6]
            slots, blocks, owner = small[:, 8:22], small[:, 24:38], small[:, 40:54]
            link(dve.tensor_copy(length, kv_i[:]))
            link(dve.tensor_scalar(small[:, 1:2], length, 1.0, None, ALU.add))
            link(dve.tensor_copy(small_i[:, 0:1], small[:, 1:2]))
            dve.tensor_scalar(small_i[:, 1:2], kv_i[:], 4, None, ALU.arith_shift_right)
            dve.tensor_scalar(small_i[:, 2:3], small_i[:, 0:1], 4, None, ALU.arith_shift_right)
            link(dve.tensor_scalar(small_i[:, 3:4], kv_i[:], BLK - 1, None, ALU.bitwise_and))
            link(dve.tensor_copy(small[:, 2:5], small_i[:, 1:4]))
            link(dve.tensor_scalar(start, small[:, 3:4], -float(WIN // BLK), 0.0, ALU.add, ALU.max))
            link(dve.tensor_scalar(start, start, float(NBLK - NR), None, ALU.min))
            dve.tensor_scalar(slots[:, 0:NE], c("ahead")[:, 0:NE], first, float(NBLK - 1), ALU.add, ALU.min)
            dve.tensor_scalar(slots[:, NE:NE + NR], c("ahead")[:, NE:NE + NR], start, None, ALU.add)
            tablef = scratch[:, 0:NBLK]
            link(dve.tensor_copy(tablef, table_i[:]))
            for k in range(NE + NR):
                ins = dve.scalar_tensor_tensor(out=scratch[:, NBLK * (k + 1):NBLK * (k + 2)], in0=c("slotno"),
                                               scalar=slots[:, k:k + 1], in1=tablef, op0=ALU.is_equal, op1=ALU.mult,
                                               accum_out=blocks[:, k:k + 1])
            link(ins)
            dve.tensor_copy(entry_i[:], blocks[:, 0:NE]).then_inc(s_blk, 1)
            for k in range(NE):
                dve.tensor_scalar(diag[:, k * B:k * B + B], ident, blocks[:, k:k + 1], None, ALU.mult)
            dve.tensor_scalar(diag[:, NE * B:], ident, length, None, ALU.mult).then_inc(s_diag, 1)
            dve.wait_ge(s_gate, 1)
            dve.scalar_tensor_tensor(out=gate_sb[:], in0=bank[3][:, 0:2 * E0], scalar=2.0, in1=gate_sb[:],
                                     op0=ALU.mult, op1=ALU.add).then_inc(s_gatec, 1)

            for st in skewed(dve, NT, 4, 1, 4):
                if st.has(1):
                    q = st.slot(1)
                    dve.wait_ge(s1_yt, st.s + 2)
                    wait(dve, s1_lg, st.s - 2)
                    dve.tensor_copy(yt[q], bank[q % 2][:, 0:D]).then_inc(s1_ytc, 1)
                if st.has(-1):
                    dve.wait_ge(s1_lg, st.s)
                    dve.tensor_copy(col(logit0, (st.s - 1) * E0, E0), bank[4 + st.slot(-1) % 2][:, 0:E0]).then_inc(s1_lgc, 1)

            def by_expert(ap, n):
                return ap.rearrange("p (i e) -> p i e", e=n)

            def spread(ap, n):
                return ap[:, :, None].broadcast_to([P, NT, n])

            buf = [route[:, 256 * k:256 * k + 256] for k in range(9)]
            b_eq, b_first, b_rest, b_second, _, b_incl, b_slot, b_prod, b_small = buf
            rev = c("rev8")[:, None, :].broadcast_to([P, NT, E0])
            dve.wait_ge(s1_lgc, NT)

            def best(logits, onehot, top):
                link(dve.tensor_reduce(top, by_expert(logits, E0), AX.X, ALU.max))
                link(dve.tensor_tensor(by_expert(b_eq, E0), by_expert(logits, E0), spread(top, E0), ALU.is_equal))
                link(dve.tensor_tensor(by_expert(b_eq, E0), by_expert(b_eq, E0), rev, ALU.mult))
                link(dve.tensor_reduce(b_small[:, 96:128], by_expert(b_eq, E0), AX.X, ALU.max))
                link(dve.tensor_tensor(by_expert(onehot, E0), rev, spread(b_small[:, 96:128], E0), ALU.is_equal))

            best(logit0[:], b_first, b_small[:, 0:32])
            link(dve.scalar_tensor_tensor(out=b_rest, in0=b_first, scalar=-1e30, in1=logit0[:], op0=ALU.mult, op1=ALU.add))
            best(b_rest, b_second, b_small[:, 32:64])
            dve.tensor_tensor(onehot0, b_first, b_second, ALU.add).then_inc(s_oh, 1)
            dve.tensor_tensor(weight[:, NT:2 * NT], b_small[:, 32:64], b_small[:, 0:32], ALU.subtract).then_inc(s_m, 1)

            def slots_of(n, turn, te_i):
                cnt, nt, end, beg = (b_small[:, 128 + 8 * k:128 + 8 * k + n] for k in range(4))
                dve.wait_ge(s_rank, turn)
                incl, total = by_expert(b_incl[:, 0:NT * n], n), by_expert(bank[7][:, 0:NT * n], n)
                for e in range(n):
                    ins = dve.tensor_tensor_scan(incl[:, :, e], c("ones")[:, 0:NT], total[:, :, e], 0.0, ALU.mult, ALU.add)
                link(ins)
                link(dve.tensor_scalar(cnt, incl[:, NT - 1, :], float(P - 1), None, ALU.add))
                link(dve.tensor_copy(small_i[:, 0:n], cnt))
                link(dve.tensor_scalar(small_i[:, 8:8 + n], small_i[:, 0:n], 7, None, ALU.arith_shift_right))
                link(dve.tensor_copy(nt, small_i[:, 8:8 + n]))
                link(dve.tensor_tensor_scan(end, c("ones")[:, 0:n], nt, 0.0, ALU.mult, ALU.add))
                link(dve.tensor_tensor(beg, end, nt, ALU.subtract))
                link(dve.tensor_scalar(beg, beg, float(P), None, ALU.mult))
                slot = by_expert(b_slot[:, 0:NT * n], n)
                link(dve.tensor_tensor(slot, incl, total, ALU.subtract))
                link(dve.tensor_tensor(b_slot[:, 0:NT * n], b_slot[:, 0:NT * n], bank[6][:, 0:NT * n], ALU.add))
                link(dve.tensor_tensor(slot, slot, beg[:, None, :].broadcast_to([P, NT, n]), ALU.add))
                link(dve.memset(tile_expert[:], 0.0))
                for e in range(n):
                    link(dve.scalar_tensor_tensor(out=tile_expert[:], in0=c("tileno"), scalar=end[:, e:e + 1],
                                                  in1=tile_expert[:], op0=ALU.is_ge, op1=ALU.add))
                link(dve.tensor_scalar(te_i[:], tile_expert[:], float(n - 1), None, ALU.min))

            def pick(onehot, n, dst):
                link(dve.tensor_tensor(b_prod[:, 0:NT * n], onehot, b_slot[:, 0:NT * n], ALU.mult))
                link(dve.tensor_reduce(b_small[:, 64:96], by_expert(b_prod[:, 0:NT * n], n), AX.X, ALU.add))
                return dve.tensor_copy(dst, b_small[:, 64:96])

            slots_of(E0, 1, te0)
            link(pick(b_first, E0, slot_i[:, 0:NT]))
            pick(b_second, E0, slot_i[:, NT:2 * NT]).then_inc(s_slot, 1)
            dve.wait_ge(s_me, 1)
            link(dve.tensor_scalar(weight[:, 0:NT], weight[:, NT:2 * NT], 1.0, None, ALU.add))
            link(dve.reciprocal(weight[:, 0:NT], weight[:, 0:NT]))
            link(dve.tensor_tensor(weight[:, NT:2 * NT], weight[:, NT:2 * NT], weight[:, 0:NT], ALU.mult))
            dve.wait_ge(s_exp0, 32)
            for e in range(E0):
                dve.wait_ge(s_fold, e + 1)
                dve.scalar_tensor_tensor(out=gup_v[:, e * 512:e * 512 + 512], in0=bank[e % 2][:, :], scalar=2.0,
                                         in1=gup_v[:, e * 512:e * 512 + 512], op0=ALU.mult, op1=ALU.add).then_inc(s_folded, 1)
                dve.scalar_tensor_tensor(out=down_v[:, e * 256:e * 256 + 256], in0=bank[2 + e % 2][:, 0:D], scalar=2.0,
                                         in1=down_v[:, e * 256:e * 256 + 256], op0=ALU.mult, op1=ALU.add).then_inc(s_folded, 1)

            dve.wait_ge(s_er, 1)
            entry_rows = scratch[:, 5888:6272]
            tokpos = index_work[:, 0:NT]
            dve.tensor_copy(entry_rows, bank[0][:, 0:NE * B])
            for j in range(BT):
                p0 = T * j
                ins = dve.tensor_scalar(tokpos[p0:p0 + T, :],
                                        bank[0][p0:p0 + T, NE * B:].rearrange("p (i j) -> p j i", j=BT)[:, j, :],
                                        c("tokmod")[p0:p0 + T, :], None, ALU.add)
            link(ins)
            for k in range(NE):
                ins = dve.tensor_scalar(later[:, k * NE * B:(k + 1) * NE * B], c("entry"), c("entry_of")[:, k:k + 1], None, ALU.is_lt)
            dve.tensor_scalar(index_work[:, 32:80], c("row48"), last_off, None, ALU.is_ge)
            link(dve.tensor_scalar(small[:, 6:7], last_off, float(T), None, ALU.add))
            for k in range(NE):
                dve.scalar_tensor_tensor(out=later[:, k * NE * B:(k + 1) * NE * B], in0=entry_rows, scalar=blocks[:, k:k + 1],
                                         in1=later[:, k * NE * B:(k + 1) * NE * B], op0=ALU.is_equal, op1=ALU.mult)
            dve.scalar_tensor_tensor(out=covers, in0=c("row48"), scalar=small[:, 6:7], in1=index_work[:, 32:80],
                                     op0=ALU.is_lt, op1=ALU.mult).then_inc(s_cmp, 1)
            match = scratch[:, 0:14 * NE * B]
            for k in range(NE + NR):
                ins = dve.scalar_tensor_tensor(out=match[:, k * NE * B:(k + 1) * NE * B], in0=entry_rows,
                                               scalar=blocks[:, k:k + 1], in1=c("entry"), op0=ALU.is_equal, op1=ALU.mult)
            link(ins)
            link(dve.tensor_reduce(owner, match.rearrange("p (k e) -> p k e", k=NE + NR), AX.X, ALU.max))
            dve.wait_ge(s_cnt, 1)
            row = index_work[:, 128:176]
            dve.tensor_scalar(index_work[:, 32:80], bank[1][:, 0:NE * BLK], 0.5, None, ALU.is_lt)
            dve.tensor_scalar(index_work[:, 176:192], c("row48")[:, 0:BLK], last_off, None, ALU.is_equal)
            link(dve.tensor_scalar(small[:, 56:59], owner[:, 0:NE], float(BLK), 1.0 - BLK, ALU.mult, ALU.add))
            for k in range(NE):
                ins = dve.tensor_scalar(row[:, BLK * k:BLK * k + BLK], c("off48")[:, BLK * k:BLK * k + BLK],
                                        small[:, 56 + k:57 + k], None, ALU.add)
            link(ins)
            link(dve.tensor_tensor(row, row, index_work[:, 32:80], ALU.mult))
            acc = [index_work[:, 192:224], index_work[:, 224:256]]
            link(dve.memset(acc[0], 0.0))
            for r in range(BLK):
                link(dve.scalar_tensor_tensor(out=acc[(r + 1) % 2], in0=row[:, r:r + T], scalar=index_work[:, 176 + r:177 + r],
                                              in1=acc[r % 2], op0=ALU.mult, op1=ALU.add))
            dve.tensor_copy(dest_b.rearrange("p (j t) -> p j t", j=BT), acc[0][:, None, :].broadcast_to([P, BT, T]))
            dve.tensor_scalar(small[:, 60:71], owner[:, NE:], 0.5, BIG, ALU.is_gt, ALU.mult)
            link(dve.tensor_scalar(small[:, 72:83], owner[:, NE:], 0.5, BIG, ALU.is_lt, ALU.mult))
            dve.scalar_tensor_tensor(out=small[:, 60:71], in0=blocks[:, NE:], scalar=8.0, in1=small[:, 60:71],
                                     op0=ALU.mult, op1=ALU.add)
            link(dve.scalar_tensor_tensor(out=small[:, 72:83], in0=owner[:, NE:], scalar=8.0, in1=small[:, 72:83],
                                          op0=ALU.mult, op1=ALU.add))
            link(dve.tensor_scalar(small[:, 72:83], small[:, 72:83], -8.0, None, ALU.add))
            for w in range(2):
                dve.tensor_tensor(read_b[:, w * KR:w * KR + KR].rearrange("p (k o) -> p k o", k=NR),
                                  small[:, 60 + 12 * w:71 + 12 * w][:, :, None].broadcast_to([P, NR, 8]),
                                  c("pair").rearrange("p (k o) -> p k o", k=NR), ALU.add)
            link(dve.scalar_tensor_tensor(out=small[:, 7:8], in0=start, scalar=float(BLK), in1=length,
                                          op0=ALU.mult, op1=ALU.subtract))
            link(dve.tensor_scalar(small[:, 7:8], small[:, 7:8], (WIN - 1) / 2, None, ALU.add))
            dve.tensor_scalar(diag[:, 0:P], ident, small[:, 7:8], None, ALU.mult).then_inc(s_turn, 1)
            dve.wait_ge(s_turned, 1)
            tokrow = index_work[:, 80:112]
            for j in range(BT):
                p0 = T * j
                ins = dve.tensor_copy(tokrow[p0:p0 + T, :],
                                      bank[2][p0:p0 + T, 0:P].rearrange("p (i j) -> p j i", j=BT)[:, j, :])
            link(ins)
            link(dve.tensor_scalar(acc[1], tokrow, 0.5, None, ALU.is_lt))
            link(dve.scalar_tensor_tensor(out=acc[0], in0=acc[1], scalar=BIG, in1=tokrow, op0=ALU.mult, op1=ALU.add))
            dve.tensor_scalar(dest_i[:], acc[0], -1.0, None, ALU.add)
            dve.tensor_copy(read_i[:], bank[2][0:KR, P:3 * P])
            dve.tensor_copy(delta[:], bank[2][:, 3 * P:]).then_inc(s_idx, 1)

            ang, turns = route[:, 0:512], route[:, 512:1024]
            dve.wait_ge(s_slot, 1)
            link(dve.tensor_tensor(ang.rearrange("p (i f) -> p i f", f=16), tokpos[:, :, None].broadcast_to([P, NT, 16]),
                                   c("freq")[:, None, :].broadcast_to([P, NT, 16]), ALU.mult))
            link(dve.tensor_scalar(turns, ang, 1.0 / TWO_PI, None, ALU.mult))
            link(dve.tensor_copy(angle_i, turns))
            link(dve.tensor_copy(turns, angle_i))
            for part in (C1, C2, C3):
                link(dve.scalar_tensor_tensor(out=ang, in0=turns, scalar=-part, in1=ang, op0=ALU.mult, op1=ALU.add))
            link(dve.tensor_scalar(cosine[:], ang, float(np.pi / 2), None, ALU.add))
            link(dve.tensor_copy(sine[:], ang))
            for a in (sine, cosine):
                link(dve.tensor_scalar(turns, a[:], float(np.pi), -TWO_PI, ALU.is_gt, ALU.mult))
                link(dve.tensor_tensor(a[:], a[:], turns, ALU.add))
                link(dve.tensor_scalar(turns, a[:], float(-np.pi), TWO_PI, ALU.is_lt, ALU.mult))
                link(dve.tensor_tensor(a[:], a[:], turns, ALU.add))
                ins = dve.tensor_scalar(a[:], a[:], 3.1415925, -3.1415925, ALU.min, ALU.max)
                if a is sine:
                    link(ins)
            ins.then_inc(s_ang, 1)

            for st in skewed(dve, N0, 4, 3, 9):
                if st.has(2):
                    q = st.slot(2) % 2
                    dve.wait_ge(s2_t, st.s + 3)
                    wait(dve, s2_g, st.s + 1)
                    dve.tensor_copy(xst[q], bank[(st.q + 1) % 2][:, 0:D]).then_inc(s2_tc, 1)
                if st.has(-1):
                    q = st.slot(-1) % 2
                    dve.wait_ge(s2_sg, st.s)
                    wait(dve, s2_ta, st.s - 2)
                    dve.tensor_tensor(ha[q], sg[q], gbank[st.slot(-1)][:, I0:2 * I0], ALU.mult).then_inc(s2_a, 1)
                if st.has(-5):
                    q = st.slot(-5)
                    dve.wait_ge(s2_d, st.s - 4)
                    wait(dve, s2_out[q], 16 * st.turn(-5))
                    dve.tensor_copy(os_[q], bank[(st.q + 1) % 2][:, D:2 * D]).then_inc(s2_dc, 1)

            dve.wait_ge(s_rope, 2)
            dve.wait_ge(s_w, 16 * 7)
            link(dve.tensor_scalar(nscale[:], nscale[:], 1.0, None, ALU.add))
            for st in skewed(dve, NT, 4, 3, 7, ch, 16):
                heads = lambda ap: ap.rearrange("p (h d) -> p h d", h=NH)
                q4, q = st.slot(-3), st.slot(-3) % 2
                if st.has(-2):
                    qm = st.slot(-2) % 2
                    dve.wait_ge(s3_sq, st.s - 1)
                    wait(dve, s3_sd, st.s - 3)
                    dve.tensor_reduce(ms[qm], heads(sq[qm]), AX.X, ALU.add).then_inc(s3_ms, 1)
                if st.has(-3):
                    dve.wait_ge(s3_sd, st.s - 2)
                    dve.wait_ge(s3_v, st.s - 2)
                    ch.mark(dve.reciprocal(rinv[q], sd[q]))
                if st.has(3):
                    qc, tile = st.slot(3), st.s + 3
                    dve.wait_ge(s3_og[qc], 32 * st.turn(3) + 32)
                    dve.wait_ge(s3_x[qc], 16 * st.turn(3) + 16)
                    wait(dve, s3_c, tile)
                    ch.mark(dve.scalar_tensor_tensor(out=x1a, in0=og[qc][0], scalar=col(weight, tile), in1=xr[qc],
                                                     op0=ALU.mult, op1=ALU.add))
                if st.has(3) or st.has(-3):
                    ch.join()
                if st.has(-3):
                    dve.tensor_tensor(heads(xn), heads(pbank[q4][:, 0:QK]), rinv[q][:, :, None].broadcast_to([P, NH, HD]),
                                      ALU.mult).then_inc(s3_xn, 1)
                if st.has(3):
                    wait(dve, s3_t, st.s)
                    wait(dve, s3_st[qc], 16 * st.turn(3))
                    dve.scalar_tensor_tensor(out=x1s[qc], in0=og[qc][1], scalar=col(weight, tile + NT), in1=x1a,
                                             op0=ALU.mult, op1=ALU.add).then_inc(s3_c, 1)
                if st.has(-3):
                    dve.wait_ge(s3_xn, st.s - 2)
                    link(dve.tensor_tensor(xg, xn, nscale[:], ALU.mult))
                    hv = lambda ap: ap.rearrange("p (h f) -> p h f", f=16)
                    for dst, tab in ((rc, cosine), (rs, sine)):
                        ins = dve.tensor_tensor(hv(dst), hv(xg), col(tab, (st.s - 3) * 16, 16)[:, None, :].broadcast_to(
                            [P, 2 * NH, 16]), ALU.mult)
                    link(ins)
                    wait(dve, s3_tq, st.s - 6)
                    wait(dve, s3_sc[q4], 16 * st.turn(-3))
                    lo, hi = (lambda ap: ap.rearrange("p (h w f) -> p h w f", h=NH, w=2)[:, :, 0, :],
                              lambda ap: ap.rearrange("p (h w f) -> p h w f", h=NH, w=2)[:, :, 1, :])
                    o = qkv[q4][:, 0:QK]
                    dve.tensor_tensor(lo(o), lo(rc), hi(rs), ALU.subtract)
                    dve.tensor_tensor(hi(o), hi(rc), lo(rs), ALU.add).then_inc(s3_qk, 1)

            stage3_drained(dve)
            dve.memset(work[:, 0:2048], 0.0).then_inc(s4_z, 1)
            counts, placed, where = b_small[:, 32:34], b_small[:, 40:44], b_small[:, 48:50]
            link(dve.memset(counts, 0.0))
            for st in skewed(dve, B, 8, 4, 11, ch, 7):
                if st.has(-2):
                    q = st.q % 2
                    dve.wait_ge(s4_ex, 2 * (st.s - 1))
                    wait(dve, s4_tp, st.s - 3)
                    dve.reciprocal(ri[q], sm[q]).then_inc(s4_ri, 1)
                if st.has(-4):
                    q = st.q % 2
                    dve.wait_ge(s4_tp, st.s - 3)
                    wait(dve, s4_pv, st.s - 5)
                    dve.tensor_copy(pt[q], bank[4 + q][0:KR, :]).then_inc(s4_tpc, 1)
                if st.has(-2):
                    q = st.q % 2
                    dve.wait_ge(s4_ri, st.s - 1)
                    for g in range(2):
                        ins = dve.tensor_scalar(pn[q][:, g * NK:g * NK + NK], pr[q][:, g * NK:g * NK + NK], ri[q][:, g:g + 1],
                                                None, ALU.mult)
                    ins.then_inc(s4_pn, 1)
                if st.has(0):
                    q = st.q % 2
                    wait(dve, s4_ex, 2 * (st.s - 1))
                    dve.wait_ge(s4_s, st.s + 1)
                    dve.wait_ge(s4_pen, st.s + 1)
                    dve.memset(guard[:], 0.0)
                    for g in range(2):
                        dve.tensor_tensor_reduce(sc[q][:, g * NK:g * NK + NK], bank[2 + q][:, g * NK:g * NK + NK], pen[q],
                                                 1.0, -3e38, ALU.add, ALU.max, mx[q][:, g:g + 1]).then_inc(s4_ttr, 1)
                if st.has(1):
                    q = st.slot(1) % 2
                    dve.wait_ge(s4_di, st.s + 2)
                    dve.tensor_scalar(pen[q], dist[q], WIN / 2, -1e30, ALU.is_gt, ALU.mult).then_inc(s4_pen, 1)
                if st.has(0):
                    q = st.q % 2
                    dve.wait_ge(s4_ttr, 2 * (st.s + 1))
                    dve.tensor_scalar(ng[q], mx[q], -SCALE, None, ALU.mult).then_inc(s4_ng, 1)
                if st.q % 4 == 0 and st.has(-9):
                    tile = 2 * st.turn(-9) + st.slot(-9) // 4
                    dve.wait_ge(s4_wc, tile + 1)
                    for e in range(E1):
                        ins = dve.scalar_tensor_tensor(out=junk[e], in0=col(rows, tile * D, D), scalar=1.0,
                                                       in1=wr1[:, e * D:e * D + D], op0=ALU.mult, op1=ALU.mult,
                                                       accum_out=col(logit1, tile * E1 + e))
                    link(ins)
                if st.q == 0 and st.has(-9):
                    g = st.turn(-9)
                    lg, oh1 = by_expert(col(logit1, g * 2 * E1, 2 * E1), E1), by_expert(onehot1, E1)
                    margin = col(b_small, g * 2, 2)
                    link(dve.tensor_tensor(margin, lg[:, :, 1], lg[:, :, 0], ALU.subtract))
                    dve.tensor_scalar(oh1[:, :, 0], margin, 0.0, None, ALU.is_le)
                    dve.tensor_scalar(oh1[:, :, 1], margin, 0.0, None, ALU.is_gt).then_inc(s_oh, 1)
                if st.q == 2 and st.has(-11):
                    g = st.turn(-11)
                    dve.wait_ge(s_rank, g + 2)
                    ranks1 = by_expert(bank[2][:, 384:384 + 2 * E1], E1)
                    link(dve.tensor_tensor(by_expert(placed, E1), ranks1, counts[:, None, :].broadcast_to([P, 2, E1]), ALU.add))
                    dve.tensor_tensor(counts, counts, bank[2][:, 400:400 + E1], ALU.add)
                    link(dve.tensor_tensor(placed, placed, onehot1, ALU.mult))
                    at0, at1 = by_expert(placed, E1)[:, :, 0], by_expert(placed, E1)[:, :, 1]
                    link(dve.scalar_tensor_tensor(out=where, in0=by_expert(onehot1, E1)[:, :, 1], scalar=float(N1 * P - 1),
                                                  in1=at0, op0=ALU.mult, op1=ALU.add))
                    link(dve.tensor_tensor(where, where, at1, ALU.subtract))
                    dve.tensor_copy(col(slot_i, 2 * NT + g * 2, 2), where).then_inc(s_slot, 1)

            dve.wait_ge(s_slot, NG + 1)
            link(dve.tensor_scalar(b_small[:, 56:57], counts[:, 0:1], 1.0 / P, None, ALU.mult))
            dve.tensor_scalar(te1[:], c("tileno"), b_small[:, 56:57], None, ALU.is_ge).then_inc(s_slot, 1)
            margin = b_small[:, 0:32]
            link(dve.tensor_scalar(weight[:, 2 * NT:], margin, -1.0, None, ALU.mult))
            dve.tensor_tensor(weight[:, 2 * NT:], weight[:, 2 * NT:], margin, ALU.min).then_inc(s_m, 1)
            dve.wait_ge(s_me, 2)
            link(dve.tensor_scalar(weight[:, 2 * NT:], weight[:, 2 * NT:], 1.0, None, ALU.add))
            link(dve.reciprocal(weight[:, 2 * NT:], weight[:, 2 * NT:]))

            for st in skewed(dve, 2 * N1, 4, 3, 4):
                if st.has(2):
                    q = st.slot(2) % 2
                    dve.wait_ge(s6_h, st.s + 3)
                    wait(dve, s6_a, st.s + 1)
                    dve.tensor_tensor(lk[q], bank[1 + q][:, :], half[q], ALU.max).then_inc(s6_l, 1)
                if st.has(1):
                    q = st.slot(1) % 2
                    dve.wait_ge(s6_ta, st.s + 2)
                    wait(dve, s6_p, st.s)
                    dve.tensor_copy(avt[q], bank[3 + q][:, :]).then_inc(s6_tac, 1)
                if st.q % 2 == 1 and st.has(0):
                    t = st.q // 2
                    dve.wait_ge(s6_p, st.s + 1)
                    wait(dve, s6_out[t], 16 * st.turn())
                    dve.tensor_copy(zs[t], bank[5 + t][:, 0:D]).then_inc(s6_pc, 1)

            for st in skewed(dve, NT, 4, 0, 4):
                if not st.has(0):
                    continue
                dve.wait_ge(s7_g[st.q], 16 * st.turn() + 16)
                dve.wait_ge(s7_x[st.q], 16 * st.turn() + 16)
                wait(dve, s7_st[st.q], 16 * st.turn())
                dve.scalar_tensor_tensor(out=res[st.q], in0=zg[st.q], scalar=col(weight, st.s + 2 * NT), in1=x1r[st.q],
                                         op0=ALU.mult, op1=ALU.add).then_inc(s7_r, 1)


def kernel(**inputs):
    import concourse.bacc as bacc
    from concourse.bass_utils import run_bass_kernel_spmd as run

    a = {k: np.asarray(v) for k, v in inputs.items()}

    def halves(w):
        return w.reshape(-1, P, w.shape[-1]).transpose(1, 0, 2).reshape(P, -1)

    consts, at = constants()
    q_order = lambda w: w.reshape(G, 2, HD, -1).transpose(1, 0, 2, 3).reshape(H * HD, -1)
    wqkv = np.concatenate([q_order(a["L1_cond_Wq"]), a["L1_cond_Wk"], a["L1_cond_Wv"]], 0)
    wo = q_order(np.ascontiguousarray(a["L1_cond_Wo"].T))
    cache = np.stack([a["L1_cond_k_blocks"], a["L1_cond_v_blocks"]], 1)
    cache = cache.transpose(0, 3, 1, 2, 4).reshape(NPHYS * BLK, 2 * KW)
    arrays = {
        "x": a["x"].reshape(B * T, D),
        "kv_lens": a["itok_B_37_3939"].reshape(B, 1),
        "table": a["itok_Bx257_0_4111"],
        "cond": a["itok_B_1_198"].reshape(B, 1),
        "consts": consts,
        "cond_w": a["L0_cond_weights"],
        "gate_t": halves(a["L0_ffn_gate_weight"].T),
        "gate_a": a["L0_ffn_gate_lora_A"],
        "gate_bt": a["L0_ffn_gate_lora_B"].T,
        "gup": a["L0_ffn_gate_up_proj"].reshape(E0, 2, P, 2 * I0).transpose(2, 0, 1, 3).reshape(P, -1),
        "down": a["L0_ffn_down_proj"].transpose(1, 0, 2).reshape(I0, -1),
        "gup_a": a["L0_ffn_gup_lora_A"].transpose(1, 0, 2).reshape(R0, -1),
        "gup_bt": a["L0_ffn_gup_lora_B"].transpose(2, 0, 1).reshape(R0, -1),
        "down_a": a["L0_ffn_down_lora_A"].transpose(1, 0, 2).reshape(R0, -1),
        "down_bt": a["L0_ffn_down_lora_B"].transpose(2, 0, 1).reshape(R0, -1),
        "wqkv": halves(wqkv.T),
        "wo": halves(wo),
        "norm_scale": norm_rows(a["L1_cond_q_norm_scale"], a["L1_cond_k_norm_scale"]),
        "cache": cache,
        "router1": np.broadcast_to(a["L1_ffn_w_router"].reshape(1, -1), (P, E1 * D)),
        "fc": a["L1_ffn_w_fc"].transpose(0, 2, 1).reshape(E1, 2, P, H1).transpose(2, 0, 1, 3).reshape(P, -1),
        "proj": a["L1_ffn_w_proj"].transpose(0, 2, 1).reshape(E1, H1 // P, P, D).transpose(2, 0, 1, 3).reshape(P, -1),
    }
    arrays = {k: np.ascontiguousarray(v) for k, v in arrays.items()}
    nc = bacc.Bacc("TRN2", target_bir_lowering=False, num_devices=1)
    args = [nc.dram_tensor(f"in_{k}", v.shape, mybir.dt.from_np(v.dtype), kind="ExternalInput").ap()
            for k, v in arrays.items()]
    out = nc.dram_tensor("out_x", (B * T, D), F32, kind="ExternalOutput").ap()
    build(nc, at, *args, out)
    r = run(nc, [{f"in_{k}": v for k, v in arrays.items()}], core_ids=[0])
    return r.results[0]["out_x"].reshape(B, T, D)


def norm_rows(q_scale, k_scale):
    row = np.concatenate([np.tile(q_scale, H), np.tile(k_scale, G)])
    return np.broadcast_to(row[None, :], (P, QK))
```
